# Optimizing a Trainium2 kernel written in Bass

```python
import numpy as np
import jax
import jax.numpy as jnp

def _softmax(x, axis=-1):
    return jax.nn.softmax(x, axis=axis)

def _gelu(x):
    return jax.nn.gelu(x, approximate=True)

def _silu(x):
    return jax.nn.silu(x)

def _sigmoid(x):
    return jax.nn.sigmoid(x)

def _layernorm(x, axis=-1, eps=1e-05):
    m = jnp.mean(x, axis=axis, keepdims=True)
    v = jnp.var(x, axis=axis, keepdims=True)
    return (x - m) / jnp.sqrt(v + eps)

def _scatter_add(tgt, idx, src, axis=0):
    return tgt.at[idx].add(src)

def _segment_sum(src, seg, n):
    return jax.ops.segment_sum(src, seg, n)
kernel_name = 'mk_sandwich_d1_jaxref_r8_8ca1ba'

def setup_inputs(seed: int=0):
    np.random.seed(seed)
    _w = jnp.asarray

    def _L0_attn_setup():
        import jax, jax.numpy as jnp
        import numpy as np
        key = jax.random.key(seed)
        k1, k2, k3, k4 = jax.random.split(key, 4)
        B, S, D_in, D_state, D_out = (8, 256, 128, 128, 128)
        x = jax.random.normal(k1, (B, S, D_in), dtype=jnp.float32)
        A = jax.random.uniform(k2, (D_state,), dtype=jnp.float32) * 0.1
        B_w = jax.random.uniform(k3, (D_state, D_in), dtype=jnp.float32, minval=-0.01, maxval=0.01)
        bound = 1.0 / np.sqrt(D_state)
        kw, kb = jax.random.split(k4)
        Wo = jax.random.uniform(kw, (D_out, D_state), dtype=jnp.float32, minval=-bound, maxval=bound)
        bo = jax.random.uniform(kb, (D_out,), dtype=jnp.float32, minval=-bound, maxval=bound)
        return {'x': x, 'A': A, 'B_w': B_w, 'Wo': Wo, 'bo': bo}
    _L0_attn_in = _L0_attn_setup()

    def _L0_ffn_setup():
        import jax, jax.numpy as jnp
        import numpy as np
        B, S, H = (2, 256, 128)
        E, I, K = (8, 512, 2)

        def _moe_forward(x, gate_w, wg, wu, wd):
            b, s, h = x.shape
            x_flat = x.reshape(-1, h)
            logits = x_flat @ gate_w.T
            top_v, top_i = jax.lax.top_k(logits, K)
            probs = jax.nn.softmax(top_v.astype(jnp.float32), axis=-1).astype(logits.dtype)
            one_hot = jax.nn.one_hot(top_i, E, dtype=probs.dtype)
            combine = jnp.einsum('tk,tke->et', probs, one_hot)

            def body(acc, ws):
                wge, wue, wde, we = ws
                hidden = jax.nn.silu(x_flat @ wge.T) * (x_flat @ wue.T)
                return (acc + we[:, None] * (hidden @ wde.T), None)
            out, _ = jax.lax.scan(body, jnp.zeros_like(x_flat), (wg, wu, wd, combine))
            return out.reshape(b, s, h)
        key = jax.random.key(seed)
        ks = jax.random.split(key, 5)
        scale_h = 1.0 / np.sqrt(H)
        scale_i = 1.0 / np.sqrt(I)
        x = jax.random.normal(ks[0], (B, S, H), dtype=jnp.float32)
        gate_w = jax.random.normal(ks[1], (E, H), dtype=jnp.float32) * scale_h
        wg = jax.random.normal(ks[2], (E, I, H), dtype=jnp.float32) * scale_h
        wu = jax.random.normal(ks[3], (E, I, H), dtype=jnp.float32) * scale_h
        wd = jax.random.normal(ks[4], (E, H, I), dtype=jnp.float32) * scale_i
        return {'x': x, 'gate_w': gate_w, 'wg': wg, 'wu': wu, 'wd': wd}
    _L0_ffn_in = _L0_ffn_setup()
    _d = {'L0_attn_x': _L0_attn_in['x'], 'L0_attn_A': _L0_attn_in['A'], 'L0_attn_B_w': _L0_attn_in['B_w'], 'L0_attn_Wo': _L0_attn_in['Wo'], 'L0_attn_bo': _L0_attn_in['bo'], 'L0_ffn_gate_w': _L0_ffn_in['gate_w'], 'L0_ffn_wg': _L0_ffn_in['wg'], 'L0_ffn_wu': _L0_ffn_in['wu'], 'L0_ffn_wd': _L0_ffn_in['wd']}
    _x0 = _d['L0_attn_x']
    _d['L0_attn_x'] = jax.random.normal(jax.random.fold_in(jax.random.key(seed), 1), (32, 256, 128), dtype=_x0.dtype)
    del _x0
    return _d

def reference(L0_attn_x, L0_attn_A, L0_attn_B_w, L0_attn_Wo, L0_attn_bo, L0_ffn_gate_w, L0_ffn_wg, L0_ffn_wu, L0_ffn_wd):

    def _L0_attn_ref(x, A, B_w, Wo, bo):
        import jax, jax.numpy as jnp
        import numpy as np
        Bsz = x.shape[0]
        D_state = A.shape[0]
        exp_decay = jnp.exp(-jnp.minimum(A, 10.0))
        Bx = jnp.einsum('bsi,ni->bsn', x, B_w)

        def step(state, bx_t):
            state = jnp.tanh(exp_decay * state + bx_t)
            return (state, state)
        init = jnp.zeros((Bsz, D_state), dtype=x.dtype)
        _, h = jax.lax.scan(step, init, jnp.swapaxes(Bx, 0, 1))
        h = jnp.swapaxes(h, 0, 1)
        out = jnp.einsum('bsn,on->bso', h, Wo) + bo
        return out

    def _L0_ffn_ref(x, gate_w, wg, wu, wd):
        import jax, jax.numpy as jnp
        import numpy as np
        B, S, H = (2, 256, 128)
        E, I, K = (8, 512, 2)

        def _moe_forward(x, gate_w, wg, wu, wd):
            b, s, h = x.shape
            x_flat = x.reshape(-1, h)
            logits = x_flat @ gate_w.T
            top_v, top_i = jax.lax.top_k(logits, K)
            probs = jax.nn.softmax(top_v.astype(jnp.float32), axis=-1).astype(logits.dtype)
            one_hot = jax.nn.one_hot(top_i, E, dtype=probs.dtype)
            combine = jnp.einsum('tk,tke->et', probs, one_hot)

            def body(acc, ws):
                wge, wue, wde, we = ws
                hidden = jax.nn.silu(x_flat @ wge.T) * (x_flat @ wue.T)
                return (acc + we[:, None] * (hidden @ wde.T), None)
            out, _ = jax.lax.scan(body, jnp.zeros_like(x_flat), (wg, wu, wd, combine))
            return out.reshape(b, s, h)
        return _moe_forward(x, gate_w, wg, wu, wd)
    x = L0_attn_x
    x = x + _layernorm(_L0_attn_ref(_layernorm(x, axis=-1), L0_attn_A, L0_attn_B_w, L0_attn_Wo, L0_attn_bo), axis=-1)
    x = x + _layernorm(_L0_ffn_ref(_layernorm(x, axis=-1), L0_ffn_gate_w, L0_ffn_wg, L0_ffn_wu, L0_ffn_wd), axis=-1)
    return x

_drawn_inputs = setup_inputs


def setup_inputs(seed=0):
    import zlib

    import numpy as np

    out = dict(_drawn_inputs(seed))
    spreads = {}
    factors = {}
    for name, (base, spread) in spreads.items():
        noise = np.random.default_rng([zlib.crc32(name.encode()), seed]).standard_normal(out[name].shape)
        drawn = base * np.exp(spread * noise) if base else spread * noise
        out[name] = jnp.asarray(drawn.astype(out[name].dtype))
    for name, factor in factors.items():
        out[name] = (out[name] * factor).astype(out[name].dtype)
    return out
```

```python
from contextlib import ExitStack

import concourse.bass as bass
from concourse import mybir

F32 = mybir.dt.float32
F32R = mybir.dt.float32r
BF16 = mybir.dt.bfloat16
I32 = mybir.dt.int32
U32 = mybir.dt.uint32
ALU = mybir.AluOpType
ACT = mybir.ActivationFunctionType
AX = mybir.AxisListType

P = 128
EPS = 1e-5


def wait_for(eng, sem, value):
    if isinstance(value, int) and value <= 0:
        return
    eng.wait_ge(sem, value)


def wait_apart(eng, settled, sem, value):
    if not isinstance(value, int):
        eng.lower_val(value)
    eng.wait_ge(settled, 1)
    eng.wait_ge(sem, value)


def in_pairs(eng, lo, hi, step):
    if lo == 0:
        step(0, 0)
        step(1, 1)
        lo = 2
    if lo < hi:
        with eng.Fori(lo // 2, hi // 2) as i:
            step(2 * i, 0)
            step(2 * i + 1, 1)


def build(nc, x, A, B_w, Wo, bo, gate_w, wg, wu, wd, out):
    NB, S, D = x.shape
    E, I, _ = wg.shape
    TPT = P // NB
    NT = S // TPT
    GT = 4
    NG = NT // GT
    NCH = 4
    GPC = NG // NCH
    IC = I // P
    NTOK = NT * P
    CAP = NTOK + P
    MT = 2 * NTOK // P + E
    SPARE = E * CAP
    ROWS = SPARE + E * P
    assert D == P and NB * TPT == P and NG % 2 == 0 and MT % 2 == 0 and I == GT * P

    x_sorted = nc.dram_tensor("x_sorted", [ROWS, D], F32, kind="Internal").ap()
    y_listed = nc.dram_tensor("y_listed", [MT * P, D], F32, kind="Internal").ap()

    ctx = ExitStack()
    with ctx:
        def sb(name, shape, dt=F32):
            return ctx.enter_context(nc.sbuf_tensor(name, shape, dt))

        def sem(name):
            return ctx.enter_context(nc.semaphore(name))

        ps = ctx.enter_context(nc.psum_tensor("ps", [P, 8, 512], F32))

        X = sb("X", [P, NT, D])
        H = sb("H", [P, NT, P])
        wg_hi, wg_lo = sb("wg_hi", [P, E * I], F32R), sb("wg_lo", [P, E * I], F32R)
        wu_hi, wu_lo = sb("wu_hi", [P, E * I], F32R), sb("wu_lo", [P, E * I], F32R)
        wd_hi, wd_lo = sb("wd_hi", [P, E * I], F32R), sb("wd_lo", [P, E * I], F32R)

        ident = sb("ident", [P, P])
        below = sb("below", [P, P], BF16)
        ones_bf = sb("ones_bf", [P, P], BF16)
        ones_f = sb("ones_f", [P, P])
        below_f = sb("below_f", [E, E])
        half = sb("half", [P, GT])
        expert_id = sb("expert_id", [P, GT, E])
        expert_row = sb("expert_row", [P, GT, E])
        tile_no = sb("tile_no", [E, MT])
        ecol = sb("ecol", [E, 2])
        tail_row = sb("tail_row", [P, E])
        decay = sb("decay", [P, 1])
        a_col = sb("a_col", [P, 1])
        bo_row = sb("bo_row", [1, D])
        BwT, WoT = sb("BwT", [P, P]), sb("WoT", [P, P])
        gateT = sb("gateT", [P, E])
        small_w = sb("small_w", [P, 2, P])
        gate_in = sb("gate_in", [E, P])

        wstage = sb("wstage", [P, 2, 512])
        xT = sb("xT", [P, 2, 512])
        tmp = sb("tmp", [P, 2, 512])
        xh2 = sb("xh2", [P, 2, 512])
        hid = sb("hid", [P, 2, 512])
        hT_hi, hT_lo = sb("hT_hi", [P, 2, 512], F32R), sb("hT_lo", [P, 2, 512], F32R)
        xeT_hi, xeT_lo = sb("xeT_hi", [P, 2, P], F32R), sb("xeT_lo", [P, 2, P], F32R)
        y_out = sb("y_out", [P, 2, D])
        u_step = ps[:, 7, :]
        st = sb("st", [P, 2, GT, 6])
        mv = sb("mv", [P, 2, GT, 2])
        ve = sb("ve", [P, 2, GT])
        rs = sb("rs", [P, 2, GT])
        nmr = sb("nmr", [P, 2, GT])
        st2 = sb("st2", [P, 2, GT, 6])
        mv2 = sb("mv2", [P, 2, GT, 2])
        ve2 = sb("ve2", [P, 2, GT])
        rs2 = sb("rs2", [P, 2, GT])
        lg = sb("lg", [P, 2, GT, E])
        mx = sb("mx", [P, 2, GT, 8])
        mi = sb("mi", [P, 2, GT, 8], U32)
        oh = sb("oh", [P, 2, 2, GT, E])
        mem = sb("mem", [P, 2, GT, E], BF16)
        gsum = sb("gsum", [P, 2, E])
        msum = sb("msum", [P, 2, E], BF16)
        rank = sb("rank", [P, 2, GT, E])
        sel = sb("sel", [P, 2, 2, GT, E])
        pos = sb("pos", [P, 2, NT], I32)
        pos_w = sb("pos_w", [P, 2, 2, GT], I32)
        margin = sb("margin", [P, NT])
        th = sb("th", [P, NT])
        prob = sb("prob", [P, 2, NT])
        tail = sb("tail", [P, E], I32)
        cnt = sb("cnt", [E, 8])
        cnt_i = sb("cnt_i", [E, 2], I32)
        tb = sb("tb", [E, 4, MT])
        tiles = sb("tiles", [1, 2, MT], I32)
        tail_i = sb("tail_i", [P, E], I32)
        shift = sb("shift", [P, E])
        pos_f, pos_y, pos_t = sb("pos_f", [P, 2 * NT]), sb("pos_y", [P, 2 * NT]), sb("pos_t", [P, 2 * NT])
        zero = sb("zero", [P, D])

        x_in = [sem(f"x_in{c}") for c in range(NCH)]
        small_in, w_in0, w_in1 = sem("small_in"), sem("w_in0"), sem("w_in1")
        w_in = (w_in0, w_in1)
        pool_k, const_ok = sem("pool_k"), sem("const_ok")
        prep_t, prep_c = sem("prep_t"), sem("prep_c")
        w_t, w_hi_ok, w_lo_ok = sem("w_t"), sem("w_hi_ok"), sem("w_lo_ok")
        ln1_st, ln1_mv, ln1_ve, ln1_rs, ln1_x = (sem("ln1_" + n) for n in ("st", "mv", "ve", "rs", "x"))
        ln1_t, ln1_xT, bx_mm, bx_ok = sem("ln1_t"), sem("ln1_xT"), sem("bx_mm"), sem("bx_ok")
        u_ok, h_ok = sem("u_ok"), sem("h_ok")
        hs_ok, o_mm, o_st, o_mv, o_ve, o_rs, o_nm, o_n, x1_ok = (
            sem("o_" + n) for n in ("hs", "mm", "st", "mv", "ve", "rs", "nm", "n", "x1"))
        l2_st, l2_mv, l2_ve, l2_rs, l2_x, l2_t, l2_xT = (
            sem("l2_" + n) for n in ("st", "mv", "ve", "rs", "x", "t", "xT"))
        lg_mm, lg_ok, mx_ok, mi_ok, oh_ok, mem_ok, gs_ok, ms_ok = (
            sem(n) for n in ("lg_mm", "lg_ok", "mx_ok", "mi_ok", "oh_ok", "mem_ok", "gs_ok", "ms_ok"))
        rk_mm, rk_ok, sel_ok, pos_ok = (sem(n) for n in ("rk_mm", "rk_ok", "sel_ok", "pos_ok"))
        pos_kept, pos_back = sem("pos_kept"), sem("pos_back")
        scat = [sem("scat0"), sem("scat1")]
        yp, tl, ypos_ok = sem("yp"), sem("tl"), sem("ypos_ok")
        fill_ok = sem("fill_ok")
        c_mm, c_ok, t_ok = sem("c_mm"), sem("c_ok"), sem("t_ok")
        tiles_mm, tiles_ok, tail_ok, tailed = sem("tiles_mm"), sem("tiles_ok"), sem("tail_ok"), sem("tailed")
        xe_in = [sem("xe_in0"), sem("xe_in1")]
        xe_t, xe_hi, xe_lo = sem("xe_t"), sem("xe_hi"), sem("xe_lo")
        gu_mm, silu_ok, hid_ok, hT_t, hT_hi_ok, hT_lo_ok = (
            sem(n) for n in ("gu_mm", "silu_ok", "hid_ok", "hT_t", "hT_hi_ok", "hT_lo_ok"))
        y_mm, y_ok = sem("y_mm"), sem("y_ok")
        y_st = [sem("y_st0"), sem("y_st1")]
        th_ok, pr_ok = sem("th_ok"), sem("pr_ok")
        gath = [sem("gath0"), sem("gath1")]
        f_a, f_b, f_st, f_mv, f_ve, f_rs, f_n, f_ok = (
            sem("f_" + n) for n in ("a", "b", "st", "mv", "ve", "rs", "n", "ok"))
        out_ok = [sem("out_ok0"), sem("out_ok1")]

        NW = 3 * E

        def tiles4(buf, u):
            return buf[:, u, :].rearrange("p (k d) -> p k d", k=GT)

        block = ctx.enter_context(nc.Block())

        @block.sync
        def _(sp):
            for c in range(NCH):
                for s in range(TPT):
                    sp.dma_start(X[s * NB:(s + 1) * NB, c * (NT // NCH):(c + 1) * (NT // NCH), :],
                                 x[:, c * (S // NCH) + s:(c + 1) * (S // NCH):TPT, :]).then_inc(x_in[c], 16)
                if c == 0:
                    sp.dma_start(small_w[:, 0, :], B_w).then_inc(small_in, 16)
                    sp.dma_start(small_w[:, 1, :], Wo).then_inc(small_in, 16)
                    sp.dma_start(gate_in[:], gate_w).then_inc(small_in, 16)
                    sp.dma_start(bo_row[:], bo.rearrange("(a d) -> a d", a=1)).then_inc(small_in, 16)
                    sp.dma_start(a_col[:], A.rearrange("(d a) -> d a", a=1)).then_inc(small_in, 16)
            for which, w in enumerate((wg, wu, wd)):
                def load(e, u, which=which, w=w):
                    n = which * E + e
                    wait_for(sp, w_t, n - 1)
                    if which < 2:
                        src = w[bass.ds(e, 1), :, :].rearrange("a (k p) d -> p (a k) d", p=P)
                    else:
                        src = w[bass.ds(e, 1), :, :].rearrange("a d (k i) -> d (a k) i", i=P)
                    sp.dma_start(tiles4(wstage, u), src).then_inc(w_in[u], 16)
                if which == 0:
                    load(0, 0)
                    load(1, 1)
                with sp.Fori(1 if which == 0 else 0, E // 2) as i:
                    load(2 * i, 0)
                    load(2 * i + 1, 1)
            sp.wait_ge(tiles_ok, 1)
            sp.wait_ge(tailed, 16 * E)
            sp.wait_ge(fill_ok, 16 * E)
            for u in range(2):
                sp.wait_ge(scat[u], 16 * 2 * GT * NG // 2)

            def rows_of(n):
                return sp.value_load(tiles[0:1, 0, bass.ds(n, 1)], min_val=0, max_val=ROWS - P)

            def load_rows(n, u):
                wait_for(sp, xe_t, n - 1)
                sp.dma_start(wstage[:, u, 0:D], x_sorted[bass.ds(rows_of(n), P), :]).then_inc(xe_in[u], 16)

            def store_rows(n, u):
                sp.wait_ge(y_ok, n + 1)
                sp.dma_start(y_listed[bass.ds(n * P, P), :], y_out[:, u, :]).then_inc(y_st[u], 16)

            load_rows(0, 0)
            load_rows(1, 1)
            with sp.Fori(1, MT // 2) as i:
                for u in range(2):
                    load_rows(2 * i + u, u)
                    store_rows(2 * i + u - 2, u)
            store_rows(MT - 2, 0)
            store_rows(MT - 1, 1)

            def store_out(g, u):
                sp.wait_ge(f_ok, g + 1)
                for s in range(TPT):
                    dst = out.rearrange("b (g t s) d -> g s b t d", t=GT, s=TPT)
                    sp.dma_start(dst[bass.ds(g, 1), s].rearrange("a b t d -> (a b) t d"),
                                 tiles4(tmp, u)[s * NB:(s + 1) * NB]).then_inc(out_ok[u], 16)
            in_pairs(sp, 0, NG, store_out)
            for u in range(2):
                sp.wait_ge(out_ok[u], 16 * TPT * NG // 2)

        @block.gpsimd
        def _(pool):
            pool.memset(ident[:], 0.0).then_inc(pool_k, 1)
            pool.memset(below[:], 0.0).then_inc(pool_k, 1)
            pool.memset(below_f[:], 0.0).then_inc(pool_k, 1)
            pool.memset(ones_bf[:], 1.0).then_inc(const_ok, 1)
            pool.memset(ones_f[:], 1.0).then_inc(const_ok, 1)
            pool.memset(half[:], -0.5).then_inc(const_ok, 1)
            pool.memset(zero[:], 0.0).then_inc(const_ok, 1)
            pool.memset(msum[:], 0.0).then_inc(const_ok, 1)
            pool.wait_ge(pool_k, 3)
            pool.affine_select(out=ident[:], in_=ident[:], compare_op=ALU.not_equal, fill=1.0, base=0,
                               pattern=[[-1, P]], channel_multiplier=1).then_inc(const_ok, 1)
            pool.affine_select(out=below[:], in_=below[:], compare_op=ALU.is_ge, fill=1.0, base=0,
                               pattern=[[-1, P]], channel_multiplier=1).then_inc(const_ok, 1)
            pool.affine_select(out=below_f[:], in_=below_f[:], compare_op=ALU.is_ge, fill=1.0, base=0,
                               pattern=[[-1, E]], channel_multiplier=1).then_inc(const_ok, 1)
            iota = dict(allow_small_or_imprecise_dtypes=True)
            pool.iota(expert_id[:], [[0, GT], [1, E]], base=0, channel_multiplier=0, **iota).then_inc(const_ok, 1)
            pool.iota(expert_row[:], [[0, GT], [CAP, E]], base=0, channel_multiplier=0, **iota).then_inc(const_ok, 1)
            pool.iota(tile_no[:], [[1, MT]], base=0, channel_multiplier=0, **iota).then_inc(const_ok, 1)
            pool.iota(ecol[:, 0:1], [[0, 1]], base=0, channel_multiplier=1, **iota).then_inc(const_ok, 1)
            pool.iota(ecol[:, 1:2], [[0, 1]], base=0, channel_multiplier=CAP, **iota).then_inc(const_ok, 1)
            pool.iota(tail_row[:], [[CAP, E]], base=0, channel_multiplier=1, **iota).then_inc(const_ok, 1)
            pool.wait_ge(const_ok, 14)
            for k in range(E):
                pool.dma_start(x_sorted[SPARE + k * P:SPARE + (k + 1) * P, :], zero[:]).then_inc(fill_ok, 16)

            def power(ve_, rs_, ready, done):
                def step(g, u):
                    pool.wait_ge(ready, g + 1)
                    pool.tensor_tensor(rs_[:, u, :], ve_[:, u, :], half[:], ALU.pow).then_inc(done, 1)
                return step

            in_pairs(pool, 0, NG, power(ve, rs, ln1_ve, ln1_rs))

            def route(g, u):
                pool.wait_ge(o_ve, g + 1)
                pool.tensor_tensor(rs[:, u, :], ve[:, u, :], half[:], ALU.pow).then_inc(o_rs, 1)
                pool.wait_ge(o_n, GT * g + GT)
                pool.tensor_tensor(X[:, bass.ds(GT * g, GT), :], X[:, bass.ds(GT * g, GT), :],
                                   tiles4(tmp, u), ALU.add).then_inc(x1_ok, 1)
                pool.wait_ge(l2_ve, g + 1)
                pool.tensor_tensor(rs2[:, u, :], ve2[:, u, :], half[:], ALU.pow).then_inc(l2_rs, 1)
                pool.wait_ge(pos_ok, g + 1)
                pool.tensor_copy(pos[:, :, bass.ds(GT * g, GT)], pos_w[:, u, :, :]).then_inc(pos_kept, 1)
                for k in range(GT):
                    for c in range(2):
                        pool.indirect_dma_start(
                            out=x_sorted, out_offset=bass.IndirectOffsetOnAxis(
                                ap=pos_w[:, u, c, k:k + 1], axis=0),
                            in_=xh2[:, u, k * P:(k + 1) * P], in_offset=None,
                            bounds_check=ROWS - 1, oob_is_err=False).then_inc(scat[u], 16)
            in_pairs(pool, 0, NG, route)

            pool.wait_ge(tail_ok, 1)
            for e in range(E):
                pool.indirect_dma_start(
                    out=x_sorted, out_offset=bass.IndirectOffsetOnAxis(ap=tail[:, e:e + 1], axis=0),
                    in_=zero[:], in_offset=None, bounds_check=ROWS - 1, oob_is_err=False).then_inc(tailed, 16)

            for u in range(2):
                pool.wait_ge(y_st[u], 16 * MT // 2)
                pool.wait_ge(scat[u], 16 * 2 * GT * NG // 2)
            pool.wait_ge(ypos_ok, 1)

            def gather(g, u):
                wait_for(pool, f_b, GT * (g - 1))
                if not isinstance(g, int):
                    pool.wait_ge(gath[u], 8 * 2 * GT * (g - u))
                pool.tensor_copy(pos_w[:, u, :, :], pos[:, :, bass.ds(GT * g, GT)]).then_inc(pos_back, 1)
                wait_apart(pool, const_ok, pos_back, g + 1)
                for k in range(GT):
                    for c, buf in enumerate((xh2, hid)):
                        pool.indirect_dma_start(
                            out=buf[:, u, k * P:(k + 1) * P], out_offset=None, in_=y_listed,
                            in_offset=bass.IndirectOffsetOnAxis(
                                ap=pos_w[:, u, c, k:k + 1], axis=0),
                            bounds_check=MT * P - 1, oob_is_err=False).then_inc(gath[u], 16)
                pool.wait_ge(f_ve, g + 1)
                pool.tensor_tensor(rs[:, u, :], ve[:, u, :], half[:], ALU.pow).then_inc(f_rs, 1)
            in_pairs(pool, 0, NG, gather)

        @block.tensor
        def _(pe):
            pe.wait_ge(const_ok, 14)
            pe.wait_ge(small_in, 16 * 5)
            pe.transpose(ps[:, 0, 0:P], small_w[:, 0, :], ident[:])
            pe.transpose(ps[:, 0, P:2 * P], small_w[:, 1, :], ident[:])
            pe.transpose(ps[:, 0, 2 * P:2 * P + E], gate_in[:], ident[0:E, 0:E]).then_inc(prep_t, 1)
            pe.wait_ge(prep_c, 4)

            def bx_group(g, u):
                pe.wait_ge(ln1_x, GT * g + GT)
                wait_for(pe, ln1_xT, g - 1)
                for k in range(GT):
                    last = pe.transpose(ps[:, u, k * P:(k + 1) * P], xT[:, u, k * P:(k + 1) * P], ident[:])
                last.then_inc(ln1_t, 1)
                pe.wait_ge(ln1_xT, g + 1)
                wait_for(pe, bx_ok, g - 1)
                pe.matmul(ps[:, 2 + u, :], BwT[:], tmp[:, u, :], start=True, stop=True).then_inc(bx_mm, 1)
            in_pairs(pe, 0, NG, bx_group)

            def weight(n, u, i):
                pe.wait_ge(w_in[u], 16 * i + 16)
                wait_for(pe, w_lo_ok, n - 1)
                for k in range(IC):
                    last = pe.transpose(ps[:, 4 + u, k * P:(k + 1) * P], wstage[:, u, k * P:(k + 1) * P], ident[:])
                last.then_inc(w_t, 1)
            weight(0, 0, 0)
            weight(1, 1, 0)
            with pe.Fori(1, NW // 2) as i:
                weight(2 * i, 0, i)
                weight(2 * i + 1, 1, i)

            def attend(g, u):
                pe.wait_ge(hs_ok, g + 1)
                wait_for(pe, o_n, GT * (g - 1))
                pe.matmul(tiles4(ps, 4 + u), ones_f[0:1, :],
                          bo_row[:].rearrange("a (k d) -> a k d", k=1).broadcast_to([1, GT, D]),
                          start=True, stop=False)
                for k in range(GT):
                    last = pe.matmul(ps[:, 4 + u, k * P:(k + 1) * P], hid[:, u, k * P:(k + 1) * P], WoT[:],
                                     start=False, stop=k == GT - 1)
                last.then_inc(o_mm, 1)
                pe.wait_ge(l2_x, GT * g + GT)
                wait_for(pe, l2_xT, g - 1)
                for k in range(GT):
                    last = pe.transpose(ps[:, u, k * P:(k + 1) * P], xh2[:, u, k * P:(k + 1) * P], ident[:])
                last.then_inc(l2_t, 1)
                pe.wait_ge(l2_xT, g + 1)
                wait_for(pe, lg_ok, g - 1)
                for k in range(GT):
                    last = pe.matmul(ps[:, 2 + u, k * E:(k + 1) * E], xT[:, u, k * P:(k + 1) * P], gateT[:],
                                     start=True, stop=True)
                last.then_inc(lg_mm, 1)
                pe.wait_ge(mem_ok, g + 1)
                wait_for(pe, ms_ok, g)
                wait_for(pe, rk_ok, g - 1)
                rk = ps[:, 6 + u, 0:GT * E].rearrange("p (k e) -> p k e", k=GT)
                pe.matmul(rk, below[:], mem[:, u, :, :], start=True, stop=False)
                pe.matmul(rk, ones_bf[:], msum[:, (1 - u):(2 - u), :].broadcast_to([P, GT, E]),
                          start=False, stop=False)
                for k in range(GT - 1):
                    last = pe.matmul(rk[:, k + 1:GT, :], ones_bf[:],
                                     mem[:, u, k:k + 1, :].broadcast_to([P, GT - 1 - k, E]),
                                     start=False, stop=k == GT - 2)
                last.then_inc(rk_mm, 1)
            in_pairs(pe, 0, NG, attend)

            pe.wait_ge(ms_ok, NG)
            pe.wait_ge(rk_ok, NG)
            pe.matmul(ps[0:E, 0, 0:1], msum[:, 1, :], ones_bf[:, 0:1], start=True, stop=True)
            pe.matmul(ps[:, 0, E:2 * E], ones_bf[:], msum[:, 1, :], start=True, stop=True).then_inc(c_mm, 1)
            pe.wait_ge(c_ok, 1)
            pe.matmul(ps[0:E, 1, 0:1], below_f[:], cnt[:, 1:2], start=True, stop=True)
            pe.matmul(ps[0:E, 1, 1:2], ones_f[0:E, 0:E], cnt[:, 1:2], start=True, stop=True).then_inc(c_mm, 1)
            pe.wait_ge(t_ok, 1)
            pe.matmul(ps[0:1, 2, 0:MT], ones_f[0:E, 0:1], tb[:, 2, :], start=True, stop=True)
            pe.matmul(ps[0:1, 3, 0:MT], ones_f[0:E, 0:1], tb[:, 3, :], start=True, stop=True).then_inc(tiles_mm, 1)
            pe.wait_ge(tiles_ok, 1)
            pe.wait_ge(w_lo_ok, NW)
            pe.wait_ge(w_hi_ok, NW)

            def t_x(n, u, i):
                pe.wait_ge(xe_in[u], 16 * i + 16)
                wait_for(pe, xe_hi, n)
                wait_for(pe, xe_lo, n)
                pe.transpose(ps[:, 6, 0:P], wstage[:, u, 0:P], ident[:]).then_inc(xe_t, 1)

            def gate_up(n, u):
                pe.wait_ge(xe_hi, n + 1)
                pe.wait_ge(xe_lo, n + 1)
                wait_for(pe, hid_ok, n - 1)
                e = pe.value_load(tiles[0:1, 1, bass.ds(n, 1)], min_val=0, max_val=E - 1)
                for b, hi, lo in ((0, wg_hi, wg_lo), (2, wu_hi, wu_lo)):
                    acc = ps[:, b + u, :]
                    pe.matmul(acc, xeT_hi[:, u, :], hi[:, bass.ds(e * I, I)], start=True, stop=False)
                    pe.matmul(acc, xeT_hi[:, u, :], lo[:, bass.ds(e * I, I)], start=False, stop=False)
                    last = pe.matmul(acc, xeT_lo[:, u, :], hi[:, bass.ds(e * I, I)], start=False, stop=True)
                last.then_inc(gu_mm, 1)

            def t_h(n, u):
                pe.wait_ge(hid_ok, n + 1)
                wait_for(pe, hT_hi_ok, n - 1)
                wait_for(pe, hT_lo_ok, n - 1)
                for k in range(IC):
                    last = pe.transpose(ps[:, 4 + u, k * P:(k + 1) * P], hid[:, u, k * P:(k + 1) * P], ident[:])
                last.then_inc(hT_t, 1)

            def down(n, u):
                pe.wait_ge(hT_hi_ok, n + 1)
                pe.wait_ge(hT_lo_ok, n + 1)
                wait_for(pe, y_ok, n)
                e = pe.value_load(tiles[0:1, 1, bass.ds(n, 1)], min_val=0, max_val=E - 1)
                for k in range(IC):
                    h, l = hT_hi[:, u, k * P:(k + 1) * P], hT_lo[:, u, k * P:(k + 1) * P]
                    pe.matmul(ps[:, 7, 0:D], h, wd_hi[:, bass.ds(e * I + k * P, P)], start=k == 0, stop=False)
                    pe.matmul(ps[:, 7, 0:D], h, wd_lo[:, bass.ds(e * I + k * P, P)], start=False, stop=False)
                    last = pe.matmul(ps[:, 7, 0:D], l, wd_hi[:, bass.ds(e * I + k * P, P)],
                                     start=False, stop=k == IC - 1)
                last.then_inc(y_mm, 1)

            t_x(0, 0, 0)
            gate_up(0, 0)
            t_x(1, 1, 0)
            gate_up(1, 1)
            t_h(0, 0)
            with pe.Fori(1, MT // 2) as i:
                for u in range(2):
                    n = 2 * i + u
                    t_x(n, u, i)
                    gate_up(n, u)
                    t_h(n - 1, 1 - u)
                    down(n - 2, u)
            t_h(MT - 1, 1)
            down(MT - 2, 0)
            down(MT - 1, 1)

        @block.scalar
        def _(act):
            act.wait_ge(prep_c, 4)
            act.activation(decay[:], a_col[:], ACT.Exp, scale=-1.0).then_inc(prep_c, 1)

            def bx_group(g, u):
                act.wait_ge(ln1_t, g + 1)
                wait_for(act, bx_mm, g - 1)
                act.copy(tmp[:, u, :], ps[:, u, :]).then_inc(ln1_xT, 1)
                act.wait_ge(bx_mm, g + 1)
                act.copy(H[:, bass.ds(GT * g, GT), :], tiles4(ps, 2 + u)).then_inc(bx_ok, 1)
            in_pairs(act, 0, NG, bx_group)

            for which, (hi) in enumerate((wg_hi, wu_hi, wd_hi)):
                def high(e, u, which=which, hi=hi):
                    act.wait_ge(w_t, which * E + e + 1)
                    act.copy(hi[:, bass.ds(e * I, I)], ps[:, 4 + u, :]).then_inc(w_hi_ok, 1)
                with act.Fori(0, E // 2) as i:
                    high(2 * i, 0)
                    high(2 * i + 1, 1)

            with act.Fori(0, S // 2) as i:
                for u in range(2):
                    act.wait_ge(u_ok, 2 * i + u + 1)
                    act.activation(H[:].rearrange("p t c -> p (t c)")[:, bass.ds((2 * i + u) * NB, NB)],
                                   ps[:, 6 + u, 0:NB], ACT.Tanh).then_inc(h_ok, 1)

            def attend(g, u):
                act.wait_ge(h_ok, TPT * GT * g + TPT * GT)
                wait_for(act, o_mm, g - 1)
                act.copy(tiles4(hid, u), H[:, bass.ds(GT * g, GT), :]).then_inc(hs_ok, 1)
                act.wait_ge(o_nm, g + 1)
                wait_for(act, x1_ok, g - 1)
                for k in range(GT):
                    act.activation(tmp[:, u, k * P:(k + 1) * P], ps[:, 4 + u, k * P:(k + 1) * P], ACT.Identity,
                                   bias=nmr[:, u, k:k + 1], scale=rs[:, u, k:k + 1]).then_inc(o_n, 1)
                act.wait_ge(l2_t, g + 1)
                wait_for(act, lg_mm, g - 1)
                act.copy(xT[:, u, :], ps[:, u, :]).then_inc(l2_xT, 1)
            in_pairs(act, 0, NG, attend)

            act.wait_ge(lg_ok, NG)
            act.wait_ge(mx_ok, GT * NG + NG)
            act.activation(th[:], margin[:], ACT.Tanh, scale=0.5).then_inc(th_ok, 1)

            def xe_high(n, u):
                act.wait_ge(xe_t, n + 1)
                wait_for(act, gu_mm, n - 1)
                act.copy(xeT_hi[:, u, :], ps[:, 6, 0:P]).then_inc(xe_hi, 1)

            def silu(n, u):
                act.wait_ge(gu_mm, n + 1)
                wait_for(act, hid_ok, n - 1)
                act.activation(tmp[:, u, :], ps[:, u, :], ACT.Silu).then_inc(silu_ok, 1)

            def hT_high(n, u):
                act.wait_ge(hT_t, n + 1)
                wait_for(act, y_mm, n - 1)
                act.copy(hT_hi[:, u, :], ps[:, 4 + u, :]).then_inc(hT_hi_ok, 1)

            xe_high(0, 0)
            silu(0, 0)
            xe_high(1, 1)
            silu(1, 1)
            hT_high(0, 0)
            with act.Fori(1, MT // 2) as i:
                for u in range(2):
                    n = 2 * i + u
                    xe_high(n, u)
                    silu(n, u)
                    hT_high(n - 1, 1 - u)
            hT_high(MT - 1, 1)

        @block.vector
        def _(dve):
            dve.wait_ge(small_in, 16 * 5)
            dve.tensor_scalar(a_col[:], a_col[:], 10.0, None, ALU.min).then_inc(prep_c, 1)
            dve.wait_ge(prep_t, 1)
            dve.tensor_copy(BwT[:], ps[:, 0, 0:P]).then_inc(prep_c, 1)
            dve.tensor_copy(WoT[:], ps[:, 0, P:2 * P]).then_inc(prep_c, 1)
            dve.tensor_copy(gateT[:], ps[:, 0, 2 * P:2 * P + E]).then_inc(prep_c, 1)

            def stats(src, g, st_, mv_, ve_, u, s_st, s_mv, s_ve):
                for k in range(GT):
                    dve.bn_stats(st_[:, u, k, :], src(k)).then_inc(s_st, 1)
                wait_apart(dve, const_ok, s_st, GT * g + GT)
                for k in range(GT):
                    dve.bn_aggr(mv_[:, u, k, :], st_[:, u, k, :]).then_inc(s_mv, 1)
                dve.wait_ge(s_mv, GT * g + GT)
                dve.tensor_scalar(ve_[:, u, :], mv_[:, u, :, 1], EPS, None, ALU.add).then_inc(s_ve, 1)

            def ln1(g, u):
                wait_for(dve, ln1_rs, g - 1)
                stats(lambda k: X[:, bass.ds(GT * g + k, 1), :], g, st, mv, ve, u, ln1_st, ln1_mv, ln1_ve)
                dve.wait_ge(ln1_rs, g + 1)
                wait_for(dve, ln1_t, g - 1)
                for k in range(GT):
                    dve.tensor_scalar(xT[:, u, k * P:(k + 1) * P], X[:, bass.ds(GT * g + k, 1), :],
                                      mv[:, u, k, 0:1], rs[:, u, k:k + 1],
                                      ALU.subtract, ALU.mult).then_inc(ln1_x, 1)
            for c in range(NCH):
                dve.wait_ge(x_in[c], 16 * TPT)
                in_pairs(dve, c * GPC, (c + 1) * GPC, ln1)

            for which, (hi, lo) in enumerate(((wg_hi, wg_lo), (wu_hi, wu_lo), (wd_hi, wd_lo))):
                def low(e, u, which=which, hi=hi, lo=lo):
                    dve.wait_ge(w_hi_ok, which * E + e + 1)
                    dve.tensor_tensor(lo[:, bass.ds(e * I, I)], ps[:, 4 + u, :],
                                      hi[:, bass.ds(e * I, I)].bitcast(F32), ALU.subtract).then_inc(w_lo_ok, 1)
                with dve.Fori(0, E // 2) as i:
                    low(2 * i, 0)
                    low(2 * i + 1, 1)

            Hf = H[:].rearrange("p t c -> p (t c)")
            dve.wait_ge(prep_c, 5)
            dve.wait_ge(bx_ok, NG)
            dve.tensor_copy(ps[:, 6, 0:NB], Hf[:, 0:NB]).then_inc(u_ok, 1)

            def linear(t, u):
                dve.wait_ge(h_ok, t)
                dve.scalar_tensor_tensor(out=ps[:, 6 + u, 0:NB], in0=Hf[:, bass.ds((t - 1) * NB, NB)],
                                         scalar=decay[:, 0:1], in1=Hf[:, bass.ds(t * NB, NB)],
                                         op0=ALU.mult, op1=ALU.add).then_inc(u_ok, 1)
            linear(1, 1)
            with dve.Fori(1, S // 2) as i:
                linear(2 * i, 0)
                linear(2 * i + 1, 1)

            def attend(g, u):
                dve.wait_ge(o_mm, g + 1)
                stats(lambda k: ps[:, 4 + u, k * P:(k + 1) * P], g, st, mv, ve, u, o_st, o_mv, o_ve)
                dve.wait_ge(o_rs, g + 1)
                dve.scalar_tensor_tensor(out=nmr[:, u, :], in0=mv[:, u, :, 0], scalar=-1.0, in1=rs[:, u, :],
                                         op0=ALU.mult, op1=ALU.mult).then_inc(o_nm, 1)
                dve.wait_ge(x1_ok, g + 1)
                stats(lambda k: X[:, bass.ds(GT * g + k, 1), :], g, st2, mv2, ve2, u, l2_st, l2_mv, l2_ve)
                dve.wait_ge(l2_rs, g + 1)
                if not isinstance(g, int):
                    dve.wait_ge(scat[u], 8 * 2 * GT * (g - u))
                for k in range(GT):
                    dve.tensor_scalar(xh2[:, u, k * P:(k + 1) * P], X[:, bass.ds(GT * g + k, 1), :],
                                      mv2[:, u, k, 0:1], rs2[:, u, k:k + 1],
                                      ALU.subtract, ALU.mult).then_inc(l2_x, 1)
                dve.wait_ge(lg_mm, g + 1)
                dve.tensor_copy(lg[:, u, :, :], ps[:, 2 + u, 0:GT * E].rearrange("p (k e) -> p k e", k=GT)
                                ).then_inc(lg_ok, 1)
                wait_apart(dve, const_ok, lg_ok, g + 1)
                for k in range(GT):
                    dve.max(out=mx[:, u, k, :], in_=lg[:, u, k, :]).then_inc(mx_ok, 1)
                wait_apart(dve, const_ok, mx_ok, (GT + 1) * g + GT)
                for k in range(GT):
                    dve.max_index(mi[:, u, k, :], mx[:, u, k, :], lg[:, u, k, :]).then_inc(mi_ok, 1)
                dve.tensor_tensor(margin[:, bass.ds(GT * g, GT)], mx[:, u, :, 0], mx[:, u, :, 1],
                                  ALU.subtract).then_inc(mx_ok, 1)
                dve.wait_ge(mi_ok, GT * g + GT)
                for c in range(2):
                    dve.tensor_tensor(oh[:, u, c, :, :], expert_id[:],
                                      mi[:, u, :, c:c + 1].broadcast_to([P, GT, E]),
                                      ALU.is_equal).then_inc(oh_ok, 1)
                dve.wait_ge(oh_ok, 2 * g + 2)
                dve.tensor_tensor(mem[:, u, :, :], oh[:, u, 0, :, :], oh[:, u, 1, :, :], ALU.add).then_inc(mem_ok, 1)
                dve.wait_ge(mem_ok, g + 1)
                dve.tensor_reduce(gsum[:, u, :], mem[:, u, :, :].rearrange("p k e -> p e k"), AX.X,
                                  ALU.add).then_inc(gs_ok, 1)
                dve.wait_ge(gs_ok, g + 1)
                wait_for(dve, ms_ok, g)
                wait_for(dve, rk_mm, g)
                dve.tensor_tensor(msum[:, u, :], gsum[:, u, :], msum[:, 1 - u, :], ALU.add).then_inc(ms_ok, 1)
                dve.wait_ge(rk_mm, g + 1)
                dve.tensor_tensor(rank[:, u, :, :], ps[:, 6 + u, 0:GT * E].rearrange("p (k e) -> p k e", k=GT),
                                  expert_row[:], ALU.add).then_inc(rk_ok, 1)
                dve.wait_ge(rk_ok, g + 1)
                for c in range(2):
                    dve.tensor_tensor(sel[:, u, c, :, :], oh[:, u, c, :, :], rank[:, u, :, :],
                                      ALU.mult).then_inc(sel_ok, 1)
                dve.wait_ge(sel_ok, 2 * g + 2)
                wait_for(dve, pos_kept, g - 1)
                with nc.allow_low_precision(reason="whole numbers below 2^24"):
                    dve.tensor_reduce(pos_w[:, u, :, :], sel[:, u, :, :, :], AX.X, ALU.add).then_inc(pos_ok, 1)
            dve.wait_ge(const_ok, 14)
            in_pairs(dve, 0, NG, attend)

            dve.wait_ge(c_mm, 1)
            cs = sem("cs")
            dve.tensor_scalar(cnt_i[:, 0:1], ps[0:E, 0, 0:1], float(P - 1), None, ALU.add).then_inc(cs, 1)
            dve.tensor_tensor(tail[:], ps[:, 0, E:2 * E], tail_row[:], ALU.add).then_inc(tail_ok, 1)
            dve.tensor_scalar(tail_i[:], ps[:, 0, E:2 * E], float(P - 1), None, ALU.add).then_inc(tl, 1)
            dve.wait_ge(tl, 1)
            dve.tensor_single_scalar(tail_i[:], tail_i[:], 7, ALU.arith_shift_right).then_inc(tl, 1)
            dve.wait_ge(tl, 2)
            dve.tensor_scalar(shift[:], tail_i[:], float(P), -float(CAP), ALU.mult, ALU.add).then_inc(tl, 1)
            dve.wait_ge(cs, 1)
            dve.tensor_single_scalar(cnt_i[:, 1:2], cnt_i[:, 0:1], 7, ALU.arith_shift_right).then_inc(cs, 1)
            dve.wait_ge(cs, 2)
            dve.tensor_copy(cnt[:, 1:2], cnt_i[:, 1:2]).then_inc(c_ok, 1)
            dve.wait_ge(c_ok, 1)
            dve.wait_ge(c_mm, 2)
            dve.tensor_copy(cnt[:, 2:3], ps[0:E, 1, 0:1]).then_inc(cs, 1)
            dve.tensor_tensor(cnt[:, 3:4], ps[0:E, 1, 0:1], cnt[:, 1:2], ALU.add).then_inc(cs, 1)
            dve.tensor_copy(cnt[:, 6:7], ps[0:E, 1, 1:2]).then_inc(cs, 1)
            dve.wait_ge(cs, 5)
            dve.scalar_tensor_tensor(out=cnt[:, 4:5], in0=cnt[:, 2:3], scalar=-float(P), in1=ecol[:, 1:2],
                                     op0=ALU.mult, op1=ALU.add).then_inc(cs, 1)
            dve.tensor_scalar(cnt[:, 5:6], cnt[:, 6:7], -float(P), float(SPARE), ALU.mult, ALU.add
                              ).then_inc(cs, 1)
            dve.tensor_scalar(tb[:, 0, :], tile_no[:], cnt[:, 2:3], None, ALU.is_ge).then_inc(cs, 1)
            dve.wait_ge(cs, 8)
            dve.scalar_tensor_tensor(out=tb[:, 1, :], in0=tile_no[:], scalar=cnt[:, 3:4], in1=tb[:, 0, :],
                                     op0=ALU.is_lt, op1=ALU.mult).then_inc(cs, 1)
            dve.tensor_scalar(tb[:, 2, :], tile_no[:], float(P), cnt[:, 4:5], ALU.mult, ALU.add).then_inc(cs, 1)
            dve.wait_ge(cs, 10)
            dve.tensor_tensor(tb[:, 2, :], tb[:, 2, :], tb[:, 1, :], ALU.mult).then_inc(cs, 1)
            dve.tensor_scalar(tb[:, 3, :], tb[:, 1, :], ecol[:, 0:1], None, ALU.mult).then_inc(cs, 1)
            dve.tensor_scalar(tb[0:1, 0, :], tile_no[0:1, :], cnt[0:1, 6:7], None, ALU.is_ge).then_inc(cs, 1)
            dve.wait_ge(cs, 13)
            dve.tensor_scalar(tb[0:1, 1, :], tile_no[0:1, :], float(P), cnt[0:1, 5:6], ALU.mult,
                              ALU.add).then_inc(cs, 1)
            dve.wait_ge(cs, 14)
            dve.tensor_tensor(tb[0:1, 1, :], tb[0:1, 1, :], tb[0:1, 0, :], ALU.mult).then_inc(cs, 1)
            dve.wait_ge(cs, 15)
            dve.tensor_tensor(tb[0:1, 2, :], tb[0:1, 2, :], tb[0:1, 1, :], ALU.add).then_inc(t_ok, 1)
            dve.wait_ge(tiles_mm, 1)
            dve.tensor_copy(tiles[:, 0, :], ps[0:1, 2, 0:MT]).then_inc(cs, 1)
            dve.wait_ge(cs, 16)
            dve.tensor_copy(tiles[:, 1, :], ps[0:1, 3, 0:MT]).then_inc(tiles_ok, 1)

            dve.wait_ge(th_ok, 1)
            dve.tensor_scalar(prob[:, 0, :], th[:], 0.5, 0.5, ALU.mult, ALU.add).then_inc(pr_ok, 1)
            dve.tensor_scalar(prob[:, 1, :], th[:], -0.5, 0.5, ALU.mult, ALU.add).then_inc(pr_ok, 1)

            dve.wait_ge(pos_kept, NG)
            dve.tensor_copy(pos_f[:], pos[:].rearrange("p c t -> p (c t)")).then_inc(yp, 1)
            dve.wait_ge(yp, 1)
            dve.wait_ge(tl, 3)
            dve.tensor_copy(pos_y[:], pos_f[:]).then_inc(yp, 1)
            for e in range(1, E):
                dve.wait_ge(yp, 2 * e)
                dve.tensor_scalar(pos_t[:], pos_f[:], float(e * CAP), shift[:, e - 1:e], ALU.is_ge,
                                  ALU.mult).then_inc(yp, 1)
                dve.wait_ge(yp, 2 * e + 1)
                dve.tensor_tensor(pos_y[:], pos_y[:], pos_t[:], ALU.add).then_inc(yp, 1)
            dve.wait_ge(yp, 2 * E)
            dve.tensor_copy(pos[:].rearrange("p c t -> p (c t)"), pos_y[:]).then_inc(ypos_ok, 1)

            def xe_low(n, u):
                dve.wait_ge(xe_hi, n + 1)
                wait_for(dve, gu_mm, n - 1)
                dve.tensor_tensor(xeT_lo[:, u, :], ps[:, 6, 0:P], xeT_hi[:, u, :].bitcast(F32),
                                  ALU.subtract).then_inc(xe_lo, 1)

            def hidden(n, u):
                dve.wait_ge(silu_ok, n + 1)
                wait_for(dve, hT_t, n - 1)
                dve.tensor_tensor(hid[:, u, :], tmp[:, u, :], ps[:, 2 + u, :], ALU.mult).then_inc(hid_ok, 1)

            def hT_low(n, u):
                dve.wait_ge(hT_hi_ok, n + 1)
                wait_for(dve, y_mm, n - 1)
                dve.tensor_tensor(hT_lo[:, u, :], ps[:, 4 + u, :], hT_hi[:, u, :].bitcast(F32),
                                  ALU.subtract).then_inc(hT_lo_ok, 1)

            def y_copy(n, u, i):
                dve.wait_ge(y_mm, n + 1)
                wait_for(dve, y_st[u], 16 * i)
                dve.tensor_copy(y_out[:, u, :], ps[:, 7, 0:D]).then_inc(y_ok, 1)

            xe_low(0, 0)
            hidden(0, 0)
            xe_low(1, 1)
            hidden(1, 1)
            hT_low(0, 0)
            with dve.Fori(1, MT // 2) as i:
                for u in range(2):
                    n = 2 * i + u
                    xe_low(n, u)
                    hidden(n, u)
                    hT_low(n - 1, 1 - u)
                    y_copy(n - 2, u, i - 1)
            hT_low(MT - 1, 1)
            y_copy(MT - 2, 0, MT // 2 - 1)
            y_copy(MT - 1, 1, MT // 2 - 1)

            dve.wait_ge(pr_ok, 2)

            def finish(g, u):
                if isinstance(g, int):
                    dve.wait_ge(gath[u], 16 * 2 * GT)
                else:
                    dve.wait_ge(gath[u], 8 * 2 * GT * (g - u) + 16 * 2 * GT)
                    dve.wait_ge(out_ok[u], 8 * TPT * (g - u))
                for k in range(GT):
                    c = slice(k * P, (k + 1) * P)
                    dve.tensor_scalar(tmp[:, u, c], xh2[:, u, c], prob[:, 0, bass.ds(GT * g + k, 1)], None,
                                      ALU.mult).then_inc(f_a, 1)
                dve.wait_ge(f_a, GT * g + GT)
                for k in range(GT):
                    c = slice(k * P, (k + 1) * P)
                    dve.scalar_tensor_tensor(out=tmp[:, u, c], in0=hid[:, u, c],
                                             scalar=prob[:, 1, bass.ds(GT * g + k, 1)], in1=tmp[:, u, c],
                                             op0=ALU.mult, op1=ALU.add).then_inc(f_b, 1)
                dve.wait_ge(f_b, GT * g + GT)
                stats(lambda k: tmp[:, u, k * P:(k + 1) * P], g, st, mv, ve, u, f_st, f_mv, f_ve)
                dve.wait_ge(f_rs, g + 1)
                for k in range(GT):
                    c = slice(k * P, (k + 1) * P)
                    dve.tensor_scalar(tmp[:, u, c], tmp[:, u, c], mv[:, u, k, 0:1], rs[:, u, k:k + 1],
                                      ALU.subtract, ALU.mult).then_inc(f_n, 1)
                dve.wait_ge(f_n, GT * g + GT)
                dve.tensor_tensor(tiles4(tmp, u), tiles4(tmp, u), X[:, bass.ds(GT * g, GT), :],
                                  ALU.add).then_inc(f_ok, 1)
            in_pairs(dve, 0, NG, finish)


_INS = ['L0_attn_x', 'L0_attn_A', 'L0_attn_B_w', 'L0_attn_Wo', 'L0_attn_bo', 'L0_ffn_gate_w',
        'L0_ffn_wg', 'L0_ffn_wu', 'L0_ffn_wd']


def kernel(**inputs):
    import numpy as _np
    import concourse.bacc as _bacc
    from concourse import mybir as _mybir
    from concourse.bass_utils import run_bass_kernel_spmd as _run

    nc = _bacc.Bacc("TRN2", target_bir_lowering=False, num_devices=1)
    arrays, args = {}, []
    for name in _INS:
        a = _np.ascontiguousarray(inputs[name])
        arrays[f"in_{name}_dram"] = a
        args.append(nc.dram_tensor(f"in_{name}_dram", a.shape, _mybir.dt.from_np(a.dtype),
                                   kind="ExternalInput").ap())
    shape = inputs['L0_attn_x'].shape
    args.append(nc.dram_tensor("out_0_dram", shape, _mybir.dt.float32, kind="ExternalOutput").ap())
    build(nc, *args)
    r = _run(nc, [arrays], core_ids=[0])
    return r.results[0]["out_0_dram"]
```

```python
from contextlib import ExitStack

import concourse.bass as bass
from concourse import mybir

F32 = mybir.dt.float32
F32R = mybir.dt.float32r
BF16 = mybir.dt.bfloat16
I32 = mybir.dt.int32
U32 = mybir.dt.uint32
ALU = mybir.AluOpType
ACT = mybir.ActivationFunctionType
AX = mybir.AxisListType

P = 128
EPS = 1e-5


def wait_for(eng, sem, value):
    if isinstance(value, int) and value <= 0:
        return
    eng.wait_ge(sem, value)


def wait_apart(eng, settled, *waits):
    waits = [w for w in waits if not isinstance(w[1], int) or w[1] > 0]
    for _, value in waits:
        if not isinstance(value, int):
            eng.lower_val(value)
    eng.wait_ge(settled, 1)
    for sem, value in waits:
        eng.wait_ge(sem, value)


def in_pairs(eng, lo, hi, step):
    if lo == 0:
        step(0, 0)
        step(1, 1)
        lo = 2
    if lo < hi:
        with eng.Fori(lo // 2, hi // 2) as i:
            step(2 * i, 0)
            step(2 * i + 1, 1)


def build(nc, x, A, B_w, Wo, bo, gate_w, w_gate, w_up, w_down, out):
    NB, S, D = x.shape
    E, I, _ = w_gate.shape
    TPT = P // NB
    NT = S // TPT
    GT = 4
    NG = NT // GT
    NCH = 4
    GPC = NG // NCH
    IC = I // P
    NTOK = NT * P
    CAP = NTOK + P
    MT = 2 * NTOK // P + E
    XB = 4
    TPE = CAP // P
    SPARE = E * CAP
    ROWS = SPARE + E * P
    assert D == P and NB * TPT == P and NG % 2 == 0 and MT % XB == 0 and XB % 2 == 0 and I == GT * P

    x_sorted = nc.dram_tensor("x_sorted", [ROWS, D], F32, kind="Internal").ap()
    y_listed = nc.dram_tensor("y_listed", [MT * P, D], F32, kind="Internal").ap()

    ctx = ExitStack()
    with ctx:
        def sb(name, shape, dt=F32):
            return ctx.enter_context(nc.sbuf_tensor(name, shape, dt))

        def sem(name):
            return ctx.enter_context(nc.semaphore(name))

        ps = ctx.enter_context(nc.psum_tensor("ps", [P, 8, 512], F32))

        X = sb("X", [P, NT, D])
        H = sb("H", [P, NT, P])
        wg_hi, wg_lo = sb("wg_hi", [P, E * I], F32R), sb("wg_lo", [P, E * I], F32R)
        wu_hi, wu_lo = sb("wu_hi", [P, E * I], F32R), sb("wu_lo", [P, E * I], F32R)
        wd = sb("wd_", [P, E * IC * 2 * D], F32R)

        ident = sb("ident", [P, P])
        below = sb("below", [P, P], BF16)
        ones_bf = sb("ones_bf", [P, P], BF16)
        ones_f = sb("ones_f", [P, P])
        below_f = sb("below_f", [E, E])
        half = sb("half", [P, GT])
        expert_id = sb("expert_id", [P, GT, E])
        expert_row = sb("expert_row", [P, GT, E])
        tile_no = sb("tile_no", [P, MT])
        eighths = sb("eighths", [1, MT // XB, XB])
        ecol = sb("ecol", [E, 2])
        tail_row = sb("tail_row", [P, E])
        decay = sb("decay", [P, 1])
        a_col = sb("a_col", [P, 1])
        bo_row = sb("bo_row", [1, D])
        BwT, WoT = sb("BwT", [P, P]), sb("WoT", [P, P])
        gateT = sb("gateT", [P, E])
        gate_in = sb("gate_in", [E, P])

        wstage = sb("wstage", [P, 2, 512])
        xT = sb("xT", [P, 2, 512])
        tmp = sb("tmp", [P, 2, 512])
        small_w = tmp[:, 1, 0:2 * P].rearrange("p (a i) -> p a i", a=2)
        xh2 = sb("xh2", [P, 2, 512])
        hid = sb("hid", [P, 2, 512])
        hT_hi, hT_lo = sb("hT_hi", [P, 2, 512], F32R), sb("hT_lo", [P, 2, 512], F32R)
        xeT_hi, xeT_lo = sb("xeT_hi", [P, 2, P], F32R), sb("xeT_lo", [P, 2, P], F32R)
        y_out = sb("y_out", [P, 2, D])
        xe = wstage[:, 0, :].rearrange("p (b d) -> p b d", b=XB)
        u_step = ps[:, 7, :]
        st = sb("st", [P, 2, GT, 6])
        mv = sb("mv", [P, 2, GT, 2])
        ve = sb("ve", [P, 2, GT])
        rs = sb("rs", [P, 2, GT])
        nmr = sb("nmr", [P, 2, GT])
        st2 = sb("st2", [P, 2, GT, 6])
        mv2 = sb("mv2", [P, 2, GT, 2])
        ve2 = sb("ve2", [P, 2, GT])
        rs2 = sb("rs2", [P, 2, GT])
        lg = sb("lg", [P, 2, GT, E])
        mx = sb("mx", [P, 2, GT, 8])
        mi = sb("mi", [P, 2, GT, 8], U32)
        oh = sb("oh", [P, 2, 2, GT, E])
        mem = sb("mem", [P, 2, GT, E], BF16)
        gsum = sb("gsum", [P, 2, E])
        msum = sb("msum", [P, 2, E], BF16)
        rank = sb("rank", [P, 2, GT, E])
        sel = sb("sel", [P, 2, 2, GT, E])
        pos = sb("pos", [P, 2, NT], I32)
        pos_w = sb("pos_w", [P, 2, 2, GT], I32)
        margin = sb("margin", [P, NT])
        th = sb("th", [P, NT])
        prob = sb("prob", [P, 2, NT])
        tail = sb("tail", [P, E], I32)
        tiles_of = sb("tiles_of", [P, E])
        tiles_e = sb("tiles_e", [E, 1])
        tiles_i = sb("tiles_i", [E, 1], I32)
        level = sb("level", [E, TPE])
        level_at = sb("level_at", [TPE, 1])
        total = sb("total", [1, 3])
        la, lb, lc, ld = (hid[0:n, h // 2, MT * (h % 2):MT * (h % 2) + MT] for h, n in enumerate((TPE, E, E, 1)))
        rows = sb("rows", [1, MT], I32)
        experts = sb("experts", [1, MT // XB], I32)
        pk = sb("pk", [1, 2, MT // XB])
        place_i = sb("place_i", [P, 2 * NT], I32)
        place_t, place_e, place_n = (sb("place_" + n, [P, 2 * NT]) for n in ("t", "e", "n"))
        pos_y = sb("pos_y", [P, 2, NT], I32)
        last_i = sb("last_i", [P, NG], I32)
        ratio = sb("ratio", [P, NT])
        fst = sb("fst", [P, 2, GT, 6])
        fmv = sb("fmv", [P, NT, 2])
        fa, fb, fv = sb("fa", [P, NT]), sb("fb", [P, NT]), sb("fv", [P, NT])
        halves = sb("halves", [P, NT])
        tail_i = sb("tail_i", [P, E], I32)
        zero = sb("zero", [P, D])

        x_in = [sem(f"x_in{c}") for c in range(NCH)]
        small_in, w_in0, w_in1 = sem("small_in"), sem("w_in0"), sem("w_in1")
        w_in = (w_in0, w_in1)
        pool_k, const_ok = sem("pool_k"), sem("const_ok")
        prep_t, prep_c = sem("prep_t"), sem("prep_c")
        w_t, w_hi_ok, w_lo_ok = sem("w_t"), sem("w_hi_ok"), sem("w_lo_ok")
        ln1_st, ln1_mv, ln1_ve, ln1_rs, ln1_x = (sem("ln1_" + n) for n in ("st", "mv", "ve", "rs", "x"))
        ln1_t, ln1_xT, bx_mm, bx_ok = sem("ln1_t"), sem("ln1_xT"), sem("bx_mm"), sem("bx_ok")
        u_ok, h_ok = sem("u_ok"), sem("h_ok")
        hs_ok, o_mm, o_st, o_mv, o_ve, o_rs, o_nm, o_n, x1_ok = (
            sem("o_" + n) for n in ("hs", "mm", "st", "mv", "ve", "rs", "nm", "n", "x1"))
        l2_st, l2_mv, l2_ve, l2_rs, l2_x, l2_t, l2_xT = (
            sem("l2_" + n) for n in ("st", "mv", "ve", "rs", "x", "t", "xT"))
        lg_mm, lg_ok, mx_ok, mi_ok, oh_ok, mem_ok, gs_ok, ms_ok = (
            sem(n) for n in ("lg_mm", "lg_ok", "mx_ok", "mi_ok", "oh_ok", "mem_ok", "gs_ok", "ms_ok"))
        rk_mm, rk_ok, sel_ok, pos_ok = (sem(n) for n in ("rk_mm", "rk_ok", "sel_ok", "pos_ok"))
        y_zero = sem("y_zero")
        pos_kept, pos_back = sem("pos_kept"), sem("pos_back")
        scat = [sem("scat0"), sem("scat1")]
        tl, pl, wide = sem("tl"), sem("pl"), sem("wide")
        fill_ok = sem("fill_ok")
        c_mm, l_ok = sem("c_mm"), sem("l_ok")
        l_mm, tiles_ok, tail_ok, tailed = sem("l_mm"), sem("tiles_ok"), sem("tail_ok"), sem("tailed")
        xe_in = [sem(f"xe_in{b}") for b in range(XB)]
        xe_t, xe_hi, xe_lo = sem("xe_t"), sem("xe_hi"), sem("xe_lo")
        gu_mm, silu_ok, hid_ok, hT_t, hT_hi_ok, hT_lo_ok = (
            sem(n) for n in ("gu_mm", "silu_ok", "hid_ok", "hT_t", "hT_hi_ok", "hT_lo_ok"))
        y_mm, y_ok = sem("y_mm"), sem("y_ok")
        y_st = [sem("y_st0"), sem("y_st1")]
        th_ok, pr_r, pr_ok = sem("th_ok"), sem("pr_r"), sem("pr_ok")
        gath = [sem("gath0"), sem("gath1")]
        f_kept = sem("f_kept")
        mix_a, mixed = sem("mix_a"), sem("mixed")
        f_st, f_mv, f_s, f_rs, f_n, f_ok = (sem("f_" + n) for n in ("st", "mv", "s", "rs", "n", "ok"))
        out_ok = [sem("out_ok0"), sem("out_ok1")]

        CONSTANTS = 15 + XB
        NW = 3 * E

        def tiles4(buf, u):
            return buf[:, u, :].rearrange("p (k d) -> p k d", k=GT)

        def wg_parts(e):
            return [w[:, bass.ds(e * I, I)].rearrange("p (k i) -> p k i", k=IC) for w in (wg_hi, wg_lo)]

        def wu_parts(e):
            return [w[:, bass.ds(e * I, I)].rearrange("p (k i) -> p k i", k=IC) for w in (wu_hi, wu_lo)]

        def wd_parts(e):
            both = wd[:, bass.ds(e * IC * 2 * D, IC * 2 * D)].rearrange("p (k h d) -> p k h d", k=IC, h=2)
            return [both[:, :, h, :] for h in range(2)]

        block = ctx.enter_context(nc.Block())

        @block.sync
        def _(sp):
            for c in range(NCH):
                for s in range(TPT):
                    sp.dma_start(X[s * NB:(s + 1) * NB, c * (NT // NCH):(c + 1) * (NT // NCH), :],
                                 x[:, c * (S // NCH) + s:(c + 1) * (S // NCH):TPT, :]).then_inc(x_in[c], 16)
                if c == 0:
                    sp.dma_start(small_w[:, 0, :], B_w).then_inc(small_in, 16)
                    sp.dma_start(small_w[:, 1, :], Wo).then_inc(small_in, 16)
                    sp.dma_start(gate_in[:], gate_w).then_inc(small_in, 16)
                    sp.dma_start(bo_row[:], bo.rearrange("(a d) -> a d", a=1)).then_inc(small_in, 16)
                    sp.dma_start(a_col[:], A.rearrange("(d a) -> d a", a=1)).then_inc(small_in, 16)
            sp.wait_ge(const_ok, CONSTANTS)
            for k in range(MT // E):
                sp.dma_start(y_listed[k * E * P:(k + 1) * E * P, :].rearrange("(a p) d -> p a d", p=P),
                             zero[:].rearrange("p (a d) -> p a d", a=1).broadcast_to([P, E, D])
                             ).then_inc(y_zero, 16)
            for which, w in enumerate((w_gate, w_up, w_down)):
                def load(e, u, which=which, w=w):
                    n = which * E + e
                    wait_for(sp, w_t, n - 1)
                    if which < 2:
                        src = w[bass.ds(e, 1), :, :].rearrange("a (k p) d -> p (a k) d", p=P)
                    else:
                        src = w[bass.ds(e, 1), :, :].rearrange("a d (k i) -> d (a k) i", i=P)
                    sp.dma_start(tiles4(wstage, u), src).then_inc(w_in[u], 16)
                if which == 0:
                    load(0, 0)
                    load(1, 1)
                with sp.Fori(1 if which == 0 else 0, E // 2) as i:
                    load(2 * i, 0)
                    load(2 * i + 1, 1)
            sp.wait_ge(w_t, NW)
            sp.wait_ge(tiles_ok, 1)
            sp.wait_ge(tailed, 16 * E)
            sp.wait_ge(fill_ok, 16 * E)
            for u in range(2):
                sp.wait_ge(scat[u], 16 * 2 * GT * NG // 2)

            def rows_of(n):
                return sp.value_load(rows[0:1, bass.ds(n, 1)], min_val=0, max_val=ROWS - P)

            def load_rows(n, b):
                wait_for(sp, xe_t, n - XB + 1)
                sp.dma_start(xe[:, b, :], x_sorted[bass.ds(rows_of(n), P), :]).then_inc(xe_in[b], 16)

            def store_rows(n, u):
                sp.wait_ge(y_ok, n + 1)
                sp.dma_start(y_listed[bass.ds(n * P, P), :], y_out[:, u, :]).then_inc(y_st[u], 16)

            sp.wait_ge(y_zero, 16 * (MT // E))
            for b in range(XB):
                load_rows(b, b)
            with sp.Fori(1, MT // XB) as i:
                for b in range(XB):
                    load_rows(XB * i + b, b)
                    store_rows(XB * i + b - XB, b % 2)
            for b in range(XB):
                store_rows(MT - XB + b, b % 2)

            def store_out(g, u):
                sp.wait_ge(f_ok, g + 1)
                for s in range(TPT):
                    dst = out.rearrange("b (g t s) d -> g s b t d", t=GT, s=TPT)
                    sp.dma_start(dst[bass.ds(g, 1), s].rearrange("a b t d -> (a b) t d"),
                                 tiles4(tmp, u)[s * NB:(s + 1) * NB]).then_inc(out_ok[u], 16)
            in_pairs(sp, 0, NG, store_out)
            for u in range(2):
                sp.wait_ge(out_ok[u], 16 * TPT * NG // 2)

        @block.gpsimd
        def _(pool):
            pool.memset(ident[:], 0.0).then_inc(pool_k, 1)
            pool.memset(below[:], 0.0).then_inc(pool_k, 1)
            pool.memset(below_f[:], 0.0).then_inc(pool_k, 1)
            pool.memset(ones_bf[:], 1.0).then_inc(const_ok, 1)
            pool.memset(ones_f[:], 1.0).then_inc(const_ok, 1)
            pool.memset(half[:], -0.5).then_inc(const_ok, 1)
            pool.memset(zero[:], 0.0).then_inc(const_ok, 1)
            pool.memset(halves[:], -0.5).then_inc(const_ok, 1)
            pool.memset(msum[:], 0.0).then_inc(const_ok, 1)
            pool.wait_ge(pool_k, 3)
            pool.affine_select(out=ident[:], in_=ident[:], compare_op=ALU.not_equal, fill=1.0, base=0,
                               pattern=[[-1, P]], channel_multiplier=1).then_inc(const_ok, 1)
            pool.affine_select(out=below[:], in_=below[:], compare_op=ALU.is_ge, fill=1.0, base=0,
                               pattern=[[-1, P]], channel_multiplier=1).then_inc(const_ok, 1)
            pool.affine_select(out=below_f[:], in_=below_f[:], compare_op=ALU.is_ge, fill=1.0, base=0,
                               pattern=[[-1, E]], channel_multiplier=1).then_inc(const_ok, 1)
            iota = dict(allow_small_or_imprecise_dtypes=True)
            pool.iota(expert_id[:], [[0, GT], [1, E]], base=0, channel_multiplier=0, **iota).then_inc(const_ok, 1)
            pool.iota(expert_row[:], [[0, GT], [CAP, E]], base=0, channel_multiplier=0, **iota).then_inc(const_ok, 1)
            pool.iota(tile_no[:], [[1, MT]], base=0, channel_multiplier=0, **iota).then_inc(const_ok, 1)
            pool.iota(ecol[:, 0:1], [[0, 1]], base=0, channel_multiplier=1, **iota).then_inc(const_ok, 1)
            pool.iota(ecol[:, 1:2], [[0, 1]], base=0, channel_multiplier=CAP, **iota).then_inc(const_ok, 1)
            pool.iota(tail_row[:], [[CAP, E]], base=0, channel_multiplier=1, **iota).then_inc(const_ok, 1)
            for b in range(XB):
                pool.memset(eighths[:, :, b], 8.0 ** b).then_inc(const_ok, 1)
            pool.wait_ge(const_ok, CONSTANTS)
            for k in range(E):
                pool.dma_start(x_sorted[SPARE + k * P:SPARE + (k + 1) * P, :], zero[:]).then_inc(fill_ok, 16)

            def power(ve_, rs_, ready, done):
                def step(g, u):
                    pool.wait_ge(ready, g + 1)
                    pool.tensor_tensor(rs_[:, u, :], ve_[:, u, :], half[:], ALU.pow).then_inc(done, 1)
                return step

            in_pairs(pool, 0, NG, power(ve, rs, ln1_ve, ln1_rs))

            def route(g, u):
                pool.wait_ge(o_ve, g + 1)
                pool.tensor_tensor(rs[:, u, :], ve[:, u, :], half[:], ALU.pow).then_inc(o_rs, 1)
                pool.wait_ge(o_n, GT * g + GT)
                pool.tensor_tensor(X[:, bass.ds(GT * g, GT), :], X[:, bass.ds(GT * g, GT), :],
                                   tiles4(tmp, u), ALU.add).then_inc(x1_ok, 1)
                pool.wait_ge(l2_ve, g + 1)
                pool.tensor_tensor(rs2[:, u, :], ve2[:, u, :], half[:], ALU.pow).then_inc(l2_rs, 1)
                pool.wait_ge(pos_ok, g + 1)
                pool.tensor_copy(pos[:, :, bass.ds(GT * g, GT)], pos_w[:, u, :, :]).then_inc(pos_kept, 1)
                for k in range(GT):
                    for c in range(2):
                        pool.indirect_dma_start(
                            out=x_sorted, out_offset=bass.IndirectOffsetOnAxis(
                                ap=pos_w[:, u, c, k:k + 1], axis=0),
                            in_=xh2[:, u, k * P:(k + 1) * P], in_offset=None,
                            bounds_check=ROWS - 1, oob_is_err=False).then_inc(scat[u], 16)
            in_pairs(pool, 0, NG, route)

            pool.wait_ge(tail_ok, 1)
            for e in range(E):
                pool.indirect_dma_start(
                    out=x_sorted, out_offset=bass.IndirectOffsetOnAxis(ap=tail[:, e:e + 1], axis=0),
                    in_=zero[:], in_offset=None, bounds_check=ROWS - 1, oob_is_err=False).then_inc(tailed, 16)

            steps = [0]

            def chained(ins):
                steps[0] += 1
                ins.then_inc(pl, 1)
                pool.wait_ge(pl, steps[0])

            va, vb = xT[:, 0, 0:2 * NT], xT[:, 0, 2 * NT:4 * NT]
            flat = pos[:].rearrange("p c t -> p (c t)")
            pool.wait_ge(pos_kept, NG)
            for u in range(2):
                pool.wait_ge(scat[u], 16 * 2 * GT * NG // 2)
            pool.wait_ge(wide, 1)
            chained(pool.tensor_scalar(place_i[:], flat, 1.0 / P, (P - 1) / (2.0 * P), ALU.mult, ALU.subtract))
            chained(pool.tensor_copy(place_t[:], place_i[:]))
            chained(pool.memset(place_e[:], 0.0))
            for e in range(1, E):
                chained(pool.tensor_scalar(va, place_t[:], float(e * TPE), None, ALU.is_ge))
                chained(pool.tensor_tensor(place_e[:], place_e[:], va, ALU.add))
            chained(pool.tensor_scalar(va, place_e[:], float(TPE), None, ALU.mult))
            chained(pool.tensor_tensor(vb, place_t[:], va, ALU.subtract))
            chained(pool.memset(place_n[:], 0.0))
            for e in range(E):
                chained(pool.tensor_scalar(va, place_e[:], float(e), None, ALU.is_gt))
                chained(pool.tensor_tensor(va, va, vb, ALU.add))
                chained(pool.tensor_scalar(va, va, tiles_of[:, e:e + 1], None, ALU.min))
                chained(pool.tensor_tensor(place_n[:], place_n[:], va, ALU.add))
            chained(pool.partition_all_reduce(place_e[:], place_n[:], P, bass.bass_isa.ReduceOp.max))
            width = 2 * NT
            while width > NG:
                if width == 2 * NT:
                    one, two = place_e[:, 0:NT], place_e[:, NT:2 * NT]
                else:
                    one, two = (place_e[:, 0:width].rearrange("p (n h) -> p n h", h=2)[:, :, h] for h in range(2))
                width //= 2
                chained(pool.tensor_tensor(va[:, 0:width], two, one, ALU.subtract))
                chained(pool.tensor_scalar(va[:, 0:width], va[:, 0:width], 0.0, None, ALU.max))
                chained(pool.tensor_tensor(vb[:, 0:width], va[:, 0:width], one, ALU.add))
                chained(pool.tensor_copy(place_e[:, 0:width], vb[:, 0:width]))
            chained(pool.tensor_scalar(last_i[:], place_e[:, 0:NG], 0.5, 0.25, ALU.mult, ALU.subtract))
            chained(pool.tensor_tensor(place_n[:], place_n[:], place_t[:], ALU.subtract))
            chained(pool.tensor_scalar(place_n[:], place_n[:], float(P), None, ALU.mult))
            chained(pool.tensor_copy(place_i[:], place_n[:]))
            chained(pool.tensor_tensor(pos_y[:].rearrange("p c t -> p (c t)"), place_i[:], flat, ALU.add))
            pool.wait_ge(pr_ok, 3)

            def gather(g, u):
                half_last = pool.value_load(last_i[0:1, bass.ds(g, 1)], min_val=0, max_val=MT // 2 - 1)
                wait_apart(pool, const_ok, (y_st[0], half_last * 16 + 16), (y_st[1], half_last * 16 + 16),
                           (gath[u], 0 if isinstance(g, int) else 8 * 2 * GT * (g - u)), (mixed, g - 1))
                pool.tensor_copy(pos_w[:, u, :, :], pos_y[:, :, bass.ds(GT * g, GT)]).then_inc(pos_back, 1)
                wait_apart(pool, const_ok, (pos_back, g + 1))
                for k in range(GT):
                    for c, buf in enumerate((xh2, xT)):
                        pool.indirect_dma_start(
                            out=buf[:, u, k * P:(k + 1) * P], out_offset=None, in_=y_listed,
                            in_offset=bass.IndirectOffsetOnAxis(ap=pos_w[:, u, c, k:k + 1], axis=0),
                            bounds_check=MT * P - 1, oob_is_err=False).then_inc(gath[u], 16)

            def mix(g, u):
                pool.wait_ge(gath[u], 8 * 2 * GT * (g - u) + 16 * 2 * GT)
                pool.tensor_tensor(tiles4(xT, u), tiles4(xT, u),
                                   ratio[:, bass.ds(GT * g, GT)].rearrange("p (k a) -> p k a", a=1)
                                   .broadcast_to([P, GT, D]), ALU.mult).then_inc(mix_a, 1)
                pool.wait_ge(mix_a, g + 1)
                pool.tensor_tensor(H[:, bass.ds(GT * g, GT), :], tiles4(xT, u), tiles4(xh2, u),
                                   ALU.add).then_inc(mixed, 1)

            gather(0, 0)
            gather(1, 1)
            mix(0, 0)
            with pool.Fori(1, NG // 2) as i:
                gather(2 * i, 0)
                mix(2 * i - 1, 1)
                gather(2 * i + 1, 1)
                mix(2 * i, 0)
            mix(NG - 1, 1)
            pool.wait_ge(f_s, 3)
            pool.tensor_tensor(fv[:], fv[:], halves[:], ALU.pow).then_inc(f_rs, 1)

        @block.tensor
        def _(pe):
            pe.wait_ge(const_ok, CONSTANTS)
            pe.wait_ge(small_in, 16 * 5)
            pe.transpose(ps[:, 0, 0:P], small_w[:, 0, :], ident[:])
            pe.transpose(ps[:, 0, P:2 * P], small_w[:, 1, :], ident[:])
            pe.transpose(ps[:, 0, 2 * P:2 * P + E], gate_in[:], ident[0:E, 0:E]).then_inc(prep_t, 1)
            pe.wait_ge(prep_c, 4)

            def bx_group(g, u):
                pe.wait_ge(ln1_x, GT * g + GT)
                wait_for(pe, ln1_xT, g - 1)
                for k in range(GT):
                    last = pe.transpose(ps[:, u, k * P:(k + 1) * P], xT[:, u, k * P:(k + 1) * P], ident[:])
                last.then_inc(ln1_t, 1)
                pe.wait_ge(ln1_xT, g + 1)
                wait_for(pe, bx_ok, g - 1)
                pe.matmul(ps[:, 2 + u, :], BwT[:], tmp[:, u, :], start=True, stop=True).then_inc(bx_mm, 1)
            in_pairs(pe, 0, NG, bx_group)

            def weight(n, u, i):
                pe.wait_ge(w_in[u], 16 * i + 16)
                wait_for(pe, w_lo_ok, n - 1)
                for k in range(IC):
                    last = pe.transpose(ps[:, 4 + u, k * P:(k + 1) * P], wstage[:, u, k * P:(k + 1) * P], ident[:])
                last.then_inc(w_t, 1)
            weight(0, 0, 0)
            weight(1, 1, 0)
            with pe.Fori(1, NW // 2) as i:
                weight(2 * i, 0, i)
                weight(2 * i + 1, 1, i)

            def attend(g, u):
                pe.wait_ge(hs_ok, g + 1)
                wait_for(pe, o_n, GT * (g - 1))
                pe.matmul(tiles4(ps, 4 + u), ones_f[0:1, :],
                          bo_row[:].rearrange("a (k d) -> a k d", k=1).broadcast_to([1, GT, D]),
                          start=True, stop=False)
                for k in range(GT):
                    last = pe.matmul(ps[:, 4 + u, k * P:(k + 1) * P], hid[:, u, k * P:(k + 1) * P], WoT[:],
                                     start=False, stop=k == GT - 1)
                last.then_inc(o_mm, 1)
                pe.wait_ge(l2_x, GT * g + GT)
                wait_for(pe, l2_xT, g - 1)
                for k in range(GT):
                    last = pe.transpose(ps[:, u, k * P:(k + 1) * P], xh2[:, u, k * P:(k + 1) * P], ident[:])
                last.then_inc(l2_t, 1)
                pe.wait_ge(l2_xT, g + 1)
                wait_for(pe, lg_ok, g - 1)
                for k in range(GT):
                    last = pe.matmul(ps[:, 2 + u, k * E:(k + 1) * E], xT[:, u, k * P:(k + 1) * P], gateT[:],
                                     start=True, stop=True)
                last.then_inc(lg_mm, 1)
                pe.wait_ge(mem_ok, g + 1)
                wait_for(pe, ms_ok, g)
                wait_for(pe, rk_ok, g - 1)
                rk = ps[:, 6 + u, 0:GT * E].rearrange("p (k e) -> p k e", k=GT)
                pe.matmul(rk, below[:], mem[:, u, :, :], start=True, stop=False)
                pe.matmul(rk, ones_bf[:], msum[:, (1 - u):(2 - u), :].broadcast_to([P, GT, E]),
                          start=False, stop=False)
                for k in range(GT - 1):
                    last = pe.matmul(rk[:, k + 1:GT, :], ones_bf[:],
                                     mem[:, u, k:k + 1, :].broadcast_to([P, GT - 1 - k, E]),
                                     start=False, stop=k == GT - 2)
                last.then_inc(rk_mm, 1)
            in_pairs(pe, 0, NG, attend)

            pe.wait_ge(ms_ok, NG)
            pe.wait_ge(rk_ok, NG)
            pe.matmul(ps[0:E, 0, 0:1], msum[:, 1, :], ones_bf[:, 0:1], start=True, stop=True)
            pe.matmul(ps[:, 0, E:2 * E], ones_bf[:], msum[:, 1, :], start=True, stop=True).then_inc(c_mm, 1)
            pe.wait_ge(l_ok, 2)
            pe.matmul(ps[0:TPE, 1, 0:1], level[:], ones_f[0:E, 0:1], start=True, stop=True)
            pe.matmul(ps[0:1, 1, 2:3], ones_f[0:E, 0:1], tiles_e[:], start=True, stop=True).then_inc(l_mm, 1)
            pe.wait_ge(l_ok, 3)
            pe.matmul(ps[0:E, 2, 0:MT], ones_f[0:TPE, 0:E], la[:], start=True, stop=True).then_inc(l_mm, 1)
            pe.wait_ge(l_ok, 5)
            pe.matmul(ps[0:E, 3, 0:MT], ones_f[0:E, 0:E], lb[:], start=True, stop=False)
            pe.matmul(ps[0:E, 3, 0:MT], below_f[:], lc[:], start=False, stop=True).then_inc(l_mm, 1)
            pe.wait_ge(l_ok, 6)
            pe.matmul(ps[0:1, 1, 4:4 + MT], ones_f[0:E, 0:1], la[0:E, :], start=True, stop=True).then_inc(l_mm, 1)
            pe.wait_ge(tiles_ok, 1)
            pe.wait_ge(w_lo_ok, NW)
            pe.wait_ge(w_hi_ok, NW)

            def t_x(n, b, i):
                pe.wait_ge(xe_in[b], 16 * i + 16)
                wait_for(pe, xe_hi, n)
                wait_for(pe, xe_lo, n)
                pe.transpose(ps[:, 6, 0:P], xe[:, b, :], ident[:]).then_inc(xe_t, 1)

            def experts_of(i):
                packed = pe.value_load(experts[0:1, bass.ds(i, 1)], min_val=0, max_val=E ** (2 * XB - 1) - 1)
                return [(packed // E ** j) % E for j in range(2 * XB - 1)]

            assert E == 8
            def gate_up(n, u, e):
                pe.wait_ge(xe_hi, n + 1)
                pe.wait_ge(xe_lo, n + 1)
                wait_for(pe, hid_ok, n - 1)
                for b, hi, lo in ((0, wg_hi, wg_lo), (2, wu_hi, wu_lo)):
                    acc = ps[:, b + u, :]
                    pe.matmul(acc, xeT_hi[:, u, :], hi[:, bass.ds(e * I, I)], start=True, stop=False)
                    pe.matmul(acc, xeT_hi[:, u, :], lo[:, bass.ds(e * I, I)], start=False, stop=False)
                    last = pe.matmul(acc, xeT_lo[:, u, :], hi[:, bass.ds(e * I, I)], start=False, stop=True)
                last.then_inc(gu_mm, 1)

            def t_h(n, u):
                pe.wait_ge(hid_ok, n + 1)
                wait_for(pe, hT_hi_ok, n - 1)
                wait_for(pe, hT_lo_ok, n - 1)
                for k in range(IC):
                    last = pe.transpose(ps[:, 4 + u, k * P:(k + 1) * P], hid[:, u, k * P:(k + 1) * P], ident[:])
                last.then_inc(hT_t, 1)

            def down(n, u, e):
                pe.wait_ge(hT_hi_ok, n + 1)
                pe.wait_ge(hT_lo_ok, n + 1)
                wait_for(pe, y_ok, n)
                for k in range(IC):
                    h, l = hT_hi[:, u, k * P:(k + 1) * P], hT_lo[:, u, k * P:(k + 1) * P]
                    pe.matmul(ps[:, 7, 0:2 * D], h, wd[:, bass.ds((e * IC + k) * 2 * D, 2 * D)],
                              start=k == 0, stop=False, skip_group_check=True)
                    last = pe.matmul(ps[:, 7, 0:D], l, wd[:, bass.ds((e * IC + k) * 2 * D, D)],
                                     start=False, stop=k == IC - 1, skip_group_check=True)
                last.then_inc(y_mm, 1)

            first = experts_of(0)
            t_x(0, 0, 0)
            gate_up(0, 0, first[3])
            t_x(1, 1, 0)
            gate_up(1, 1, first[4])
            t_x(2, 2, 0)
            t_h(0, 0)
            gate_up(2, 0, first[5])
            t_x(3, 3, 0)
            t_h(1, 1)
            down(0, 0, first[3])
            gate_up(3, 1, first[6])
            with pe.Fori(1, MT // XB) as i:
                listed = experts_of(i)
                for b in range(XB):
                    n = XB * i + b
                    t_x(n, b, i)
                    t_h(n - 2, b % 2)
                    down(n - 3, 1 - b % 2, listed[b])
                    gate_up(n, b % 2, listed[b + 3])
            final = experts_of(MT // XB - 1)
            t_h(MT - 2, 0)
            down(MT - 3, 1, final[4])
            t_h(MT - 1, 1)
            down(MT - 2, 0, final[5])
            down(MT - 1, 1, final[6])

        @block.scalar
        def _(act):
            act.wait_ge(prep_c, 4)
            act.activation(decay[:], a_col[:], ACT.Exp, scale=-1.0).then_inc(prep_c, 1)

            def bx_group(g, u):
                act.wait_ge(ln1_t, g + 1)
                wait_for(act, bx_mm, g - 1)
                act.copy(tmp[:, u, :], ps[:, u, :]).then_inc(ln1_xT, 1)
                act.wait_ge(bx_mm, g + 1)
                act.copy(H[:, bass.ds(GT * g, GT), :], tiles4(ps, 2 + u)).then_inc(bx_ok, 1)
            in_pairs(act, 0, NG, bx_group)

            for which, parts in enumerate((wg_parts, wu_parts, wd_parts)):
                def high(e, u, which=which, parts=parts):
                    act.wait_ge(w_t, which * E + e + 1)
                    act.copy(parts(e)[0], tiles4(ps, 4 + u)).then_inc(w_hi_ok, 1)
                with act.Fori(0, E // 2) as i:
                    high(2 * i, 0)
                    high(2 * i + 1, 1)

            with act.Fori(0, S // 2) as i:
                for u in range(2):
                    act.wait_ge(u_ok, 2 * i + u + 1)
                    act.activation(H[:].rearrange("p t c -> p (t c)")[:, bass.ds((2 * i + u) * NB, NB)],
                                   ps[:, 6 + u, 0:NB], ACT.Tanh).then_inc(h_ok, 1)

            def attend(g, u):
                act.wait_ge(h_ok, TPT * GT * g + TPT * GT)
                wait_for(act, o_mm, g - 1)
                act.copy(tiles4(hid, u), H[:, bass.ds(GT * g, GT), :]).then_inc(hs_ok, 1)
                act.wait_ge(o_nm, g + 1)
                wait_for(act, x1_ok, g - 1)
                for k in range(GT):
                    act.activation(tmp[:, u, k * P:(k + 1) * P], ps[:, 4 + u, k * P:(k + 1) * P], ACT.Identity,
                                   bias=nmr[:, u, k:k + 1], scale=rs[:, u, k:k + 1]).then_inc(o_n, 1)
                act.wait_ge(l2_t, g + 1)
                wait_for(act, lg_mm, g - 1)
                act.copy(xT[:, u, :], ps[:, u, :]).then_inc(l2_xT, 1)
            in_pairs(act, 0, NG, attend)

            act.wait_ge(lg_ok, NG)
            act.wait_ge(mx_ok, GT * NG + NG)
            act.activation(th[:], margin[:], ACT.Tanh, scale=0.5).then_inc(th_ok, 1)

            def xe_high(n, u):
                act.wait_ge(xe_t, n + 1)
                wait_for(act, gu_mm, n - 1)
                act.copy(xeT_hi[:, u, :], ps[:, 6, 0:P]).then_inc(xe_hi, 1)

            def silu(n, u):
                act.wait_ge(gu_mm, n + 1)
                wait_for(act, hid_ok, n - 1)
                act.activation(tmp[:, u, :], ps[:, u, :], ACT.Silu).then_inc(silu_ok, 1)

            def hT_high(n, u):
                act.wait_ge(hT_t, n + 1)
                wait_for(act, y_mm, n - 1)
                act.copy(hT_hi[:, u, :], ps[:, 4 + u, :]).then_inc(hT_hi_ok, 1)

            xe_high(0, 0)
            silu(0, 0)
            xe_high(1, 1)
            silu(1, 1)
            for n in (2, 3):
                xe_high(n, n % 2)
                hT_high(n - 2, n % 2)
                silu(n, n % 2)
            with act.Fori(2, MT // 2) as i:
                for u in range(2):
                    n = 2 * i + u
                    xe_high(n, u)
                    hT_high(n - 2, u)
                    silu(n, u)
            hT_high(MT - 2, 0)
            hT_high(MT - 1, 1)

            act.wait_ge(f_s, 5)

            def finish(g, u):
                if not isinstance(g, int):
                    act.wait_ge(out_ok[u], 8 * TPT * (g - u))
                for k in range(GT):
                    act.activation(tmp[:, u, k * P:(k + 1) * P], H[:, bass.ds(GT * g + k, 1), :], ACT.Identity,
                                   bias=fb[:, bass.ds(GT * g + k, 1)],
                                   scale=fa[:, bass.ds(GT * g + k, 1)]).then_inc(f_n, 1)
            in_pairs(act, 0, NG, finish)

        @block.vector
        def _(dve):
            dve.wait_ge(small_in, 16 * 5)
            dve.tensor_scalar(a_col[:], a_col[:], 10.0, None, ALU.min).then_inc(prep_c, 1)
            dve.wait_ge(prep_t, 1)
            dve.tensor_copy(BwT[:], ps[:, 0, 0:P]).then_inc(prep_c, 1)
            dve.tensor_copy(WoT[:], ps[:, 0, P:2 * P]).then_inc(prep_c, 1)
            dve.tensor_copy(gateT[:], ps[:, 0, 2 * P:2 * P + E]).then_inc(prep_c, 1)

            def stats(src, g, st_, mv_, ve_, u, s_st, s_mv, s_ve):
                for k in range(GT):
                    dve.bn_stats(st_[:, u, k, :], src(k)).then_inc(s_st, 1)
                wait_apart(dve, const_ok, (s_st, GT * g + GT))
                for k in range(GT):
                    dve.bn_aggr(mv_[:, u, k, :], st_[:, u, k, :]).then_inc(s_mv, 1)
                dve.wait_ge(s_mv, GT * g + GT)
                dve.tensor_scalar(ve_[:, u, :], mv_[:, u, :, 1], EPS, None, ALU.add).then_inc(s_ve, 1)

            def ln1(g, u):
                wait_for(dve, ln1_rs, g - 1)
                stats(lambda k: X[:, bass.ds(GT * g + k, 1), :], g, st, mv, ve, u, ln1_st, ln1_mv, ln1_ve)
                dve.wait_ge(ln1_rs, g + 1)
                wait_for(dve, ln1_t, g - 1)
                for k in range(GT):
                    dve.tensor_scalar(xT[:, u, k * P:(k + 1) * P], X[:, bass.ds(GT * g + k, 1), :],
                                      mv[:, u, k, 0:1], rs[:, u, k:k + 1],
                                      ALU.subtract, ALU.mult).then_inc(ln1_x, 1)
            for c in range(NCH):
                dve.wait_ge(x_in[c], 16 * TPT)
                in_pairs(dve, c * GPC, (c + 1) * GPC, ln1)

            for which, parts in enumerate((wg_parts, wu_parts, wd_parts)):
                def low(e, u, which=which, parts=parts):
                    dve.wait_ge(w_hi_ok, which * E + e + 1)
                    hi, lo = parts(e)
                    dve.tensor_tensor(lo, tiles4(ps, 4 + u), hi.bitcast(F32), ALU.subtract).then_inc(w_lo_ok, 1)
                with dve.Fori(0, E // 2) as i:
                    low(2 * i, 0)
                    low(2 * i + 1, 1)

            Hf = H[:].rearrange("p t c -> p (t c)")
            dve.wait_ge(prep_c, 5)
            dve.wait_ge(bx_ok, NG)
            dve.tensor_copy(ps[:, 6, 0:NB], Hf[:, 0:NB]).then_inc(u_ok, 1)

            def linear(t, u):
                dve.wait_ge(h_ok, t)
                dve.scalar_tensor_tensor(out=ps[:, 6 + u, 0:NB], in0=Hf[:, bass.ds((t - 1) * NB, NB)],
                                         scalar=decay[:, 0:1], in1=Hf[:, bass.ds(t * NB, NB)],
                                         op0=ALU.mult, op1=ALU.add).then_inc(u_ok, 1)
            linear(1, 1)
            with dve.Fori(1, S // 2) as i:
                linear(2 * i, 0)
                linear(2 * i + 1, 1)

            def attend(g, u):
                dve.wait_ge(o_mm, g + 1)
                stats(lambda k: ps[:, 4 + u, k * P:(k + 1) * P], g, st, mv, ve, u, o_st, o_mv, o_ve)
                dve.wait_ge(o_rs, g + 1)
                dve.scalar_tensor_tensor(out=nmr[:, u, :], in0=mv[:, u, :, 0], scalar=-1.0, in1=rs[:, u, :],
                                         op0=ALU.mult, op1=ALU.mult).then_inc(o_nm, 1)
                dve.wait_ge(x1_ok, g + 1)
                stats(lambda k: X[:, bass.ds(GT * g + k, 1), :], g, st2, mv2, ve2, u, l2_st, l2_mv, l2_ve)
                dve.wait_ge(l2_rs, g + 1)
                if not isinstance(g, int):
                    dve.wait_ge(scat[u], 8 * 2 * GT * (g - u))
                for k in range(GT):
                    dve.tensor_scalar(xh2[:, u, k * P:(k + 1) * P], X[:, bass.ds(GT * g + k, 1), :],
                                      mv2[:, u, k, 0:1], rs2[:, u, k:k + 1],
                                      ALU.subtract, ALU.mult).then_inc(l2_x, 1)
                dve.wait_ge(lg_mm, g + 1)
                dve.tensor_copy(lg[:, u, :, :], ps[:, 2 + u, 0:GT * E].rearrange("p (k e) -> p k e", k=GT)
                                ).then_inc(lg_ok, 1)
                wait_apart(dve, const_ok, (lg_ok, g + 1))
                for k in range(GT):
                    dve.max(out=mx[:, u, k, :], in_=lg[:, u, k, :]).then_inc(mx_ok, 1)
                wait_apart(dve, const_ok, (mx_ok, (GT + 1) * g + GT))
                for k in range(GT):
                    dve.max_index(mi[:, u, k, :], mx[:, u, k, :], lg[:, u, k, :]).then_inc(mi_ok, 1)
                dve.tensor_tensor(margin[:, bass.ds(GT * g, GT)], mx[:, u, :, 0], mx[:, u, :, 1],
                                  ALU.subtract).then_inc(mx_ok, 1)
                dve.wait_ge(mi_ok, GT * g + GT)
                for c in range(2):
                    dve.tensor_tensor(oh[:, u, c, :, :], expert_id[:],
                                      mi[:, u, :, c:c + 1].broadcast_to([P, GT, E]),
                                      ALU.is_equal).then_inc(oh_ok, 1)
                dve.wait_ge(oh_ok, 2 * g + 2)
                dve.tensor_tensor(mem[:, u, :, :], oh[:, u, 0, :, :], oh[:, u, 1, :, :], ALU.add).then_inc(mem_ok, 1)
                dve.wait_ge(mem_ok, g + 1)
                dve.tensor_reduce(gsum[:, u, :], mem[:, u, :, :].rearrange("p k e -> p e k"), AX.X,
                                  ALU.add).then_inc(gs_ok, 1)
                dve.wait_ge(gs_ok, g + 1)
                wait_for(dve, ms_ok, g)
                wait_for(dve, rk_mm, g)
                dve.tensor_tensor(msum[:, u, :], gsum[:, u, :], msum[:, 1 - u, :], ALU.add).then_inc(ms_ok, 1)
                dve.wait_ge(rk_mm, g + 1)
                dve.tensor_tensor(rank[:, u, :, :], ps[:, 6 + u, 0:GT * E].rearrange("p (k e) -> p k e", k=GT),
                                  expert_row[:], ALU.add).then_inc(rk_ok, 1)
                dve.wait_ge(rk_ok, g + 1)
                for c in range(2):
                    dve.tensor_tensor(sel[:, u, c, :, :], oh[:, u, c, :, :], rank[:, u, :, :],
                                      ALU.mult).then_inc(sel_ok, 1)
                dve.wait_ge(sel_ok, 2 * g + 2)
                wait_for(dve, pos_kept, g - 1)
                with nc.allow_low_precision(reason="whole numbers below 2^24"):
                    dve.tensor_reduce(pos_w[:, u, :, :], sel[:, u, :, :, :], AX.X, ALU.add).then_inc(pos_ok, 1)
            dve.wait_ge(const_ok, CONSTANTS)
            in_pairs(dve, 0, NG, attend)

            steps = [0]

            def chained(ins):
                steps[0] += 1
                ins.then_inc(tl, 1)
                dve.wait_ge(tl, steps[0])

            dve.wait_ge(c_mm, 1)
            dve.tensor_tensor(tail[:], ps[:, 0, E:2 * E], tail_row[:], ALU.add).then_inc(tail_ok, 1)
            chained(dve.tensor_scalar(tiles_i[:], ps[0:E, 0, 0:1], float(P - 1), None, ALU.add))
            chained(dve.tensor_single_scalar(tiles_i[:], tiles_i[:], 7, ALU.arith_shift_right))
            dve.tensor_copy(tiles_e[:], tiles_i[:]).then_inc(l_ok, 1)
            dve.wait_ge(l_ok, 1)
            dve.tensor_scalar(level[:], tile_no[0:E, 0:TPE], tiles_e[:, 0:1], None, ALU.min).then_inc(l_ok, 1)
            chained(dve.tensor_scalar(tail_i[:], ps[:, 0, E:2 * E], float(P - 1), None, ALU.add))
            chained(dve.tensor_single_scalar(tail_i[:], tail_i[:], 7, ALU.arith_shift_right))
            dve.tensor_copy(tiles_of[:], tail_i[:]).then_inc(wide, 1)
            dve.wait_ge(l_mm, 1)
            chained(dve.tensor_copy(total[:, 0:1], ps[0:1, 1, 2:3]))
            chained(dve.tensor_copy(level_at[:], ps[0:TPE, 1, 0:1]))
            dve.tensor_scalar(la[:], tile_no[0:TPE, :], level_at[:, 0:1], None, ALU.is_ge).then_inc(l_ok, 1)
            dve.wait_ge(l_mm, 2)
            dve.tensor_scalar(lb[:], ps[0:E, 2, 0:MT], -1.0, tiles_e[:, 0:1], ALU.add, ALU.min).then_inc(l_ok, 1)
            dve.tensor_scalar(lc[:], ps[0:E, 2, 0:MT], -1.0, tiles_e[:, 0:1], ALU.add, ALU.is_lt).then_inc(l_ok, 1)
            chained(dve.tensor_scalar(ld[:], ps[0:1, 2, 0:MT], float(P), -float(P), ALU.mult, ALU.add))
            dve.wait_ge(l_mm, 3)
            dve.tensor_tensor(la[0:E, :], ps[0:E, 3, 0:MT], tile_no[0:E, :], ALU.is_le).then_inc(l_ok, 1)
            chained(dve.tensor_scalar(total[:, 1:2], total[:, 0:1], -float(P), float(SPARE), ALU.mult, ALU.add))
            chained(dve.tensor_scalar(lb[0:1, :], tile_no[0:1, :], float(P), total[:, 1:2], ALU.mult, ALU.add))
            chained(dve.tensor_scalar(lc[0:1, :], tile_no[0:1, :], total[:, 0:1], None, ALU.is_lt))
            chained(dve.tensor_tensor(ld[:], ld[:], lb[0:1, :], ALU.subtract))
            dve.wait_ge(l_mm, 4)
            chained(dve.tensor_scalar(la[0:1, :], ps[0:1, 1, 4:4 + MT], -1.0, None, ALU.add))
            chained(dve.scalar_tensor_tensor(out=ld[:], in0=la[0:1, :], scalar=float(CAP), in1=ld[:],
                                             op0=ALU.mult, op1=ALU.add))
            chained(dve.tensor_tensor(ld[:], ld[:], lc[0:1, :], ALU.mult))
            chained(dve.tensor_tensor(rows[:], ld[:], lb[0:1, :], ALU.add))
            four = la[0:1, :].rearrange("p (i b) -> p i b", b=XB)
            chained(dve.tensor_tensor(ld[:].rearrange("p (i b) -> p i b", b=XB), four, eighths[:], ALU.mult))
            chained(dve.tensor_reduce(pk[:, 0, :], ld[:].rearrange("p (i b) -> p i b", b=XB), AX.X, ALU.add))
            chained(dve.tensor_tensor(pk[:, 1, :], pk[:, 0, :], four[:, :, 0], ALU.subtract))
            chained(dve.tensor_scalar(pk[:, 1, :], pk[:, 1, :], 1.0 / E, None, ALU.mult))
            chained(dve.tensor_scalar(pk[:, 0, :], pk[:, 0, :], float(E ** 3), None, ALU.mult))
            chained(dve.tensor_copy(experts[:, 0:1], pk[:, 0, 0:1]))
            dve.tensor_tensor(experts[:, 1:], pk[:, 0, 1:], pk[:, 1, 0:MT // XB - 1], ALU.add).then_inc(tiles_ok, 1)

            dve.wait_ge(th_ok, 1)
            dve.tensor_scalar(prob[:, 0, :], th[:], 0.5, 0.5, ALU.mult, ALU.add).then_inc(pr_ok, 1)
            dve.tensor_scalar(prob[:, 1, :], th[:], -0.5, 0.5, ALU.mult, ALU.add).then_inc(pr_ok, 1)
            dve.wait_ge(pr_ok, 2)
            dve.reciprocal(ratio[:], prob[:, 0, :]).then_inc(pr_r, 1)
            dve.wait_ge(pr_r, 1)
            dve.tensor_tensor(ratio[:], ratio[:], prob[:, 1, :], ALU.mult).then_inc(pr_ok, 1)

            def xe_low(n, u):
                dve.wait_ge(xe_hi, n + 1)
                wait_for(dve, gu_mm, n - 1)
                dve.tensor_tensor(xeT_lo[:, u, :], ps[:, 6, 0:P], xeT_hi[:, u, :].bitcast(F32),
                                  ALU.subtract).then_inc(xe_lo, 1)

            def hidden(n, u):
                dve.wait_ge(silu_ok, n + 1)
                wait_for(dve, hT_t, n - 1)
                dve.tensor_tensor(hid[:, u, :], tmp[:, u, :], ps[:, 2 + u, :], ALU.mult).then_inc(hid_ok, 1)

            def hT_low(n, u):
                dve.wait_ge(hT_hi_ok, n + 1)
                wait_for(dve, y_mm, n - 1)
                dve.tensor_tensor(hT_lo[:, u, :], ps[:, 4 + u, :], hT_hi[:, u, :].bitcast(F32),
                                  ALU.subtract).then_inc(hT_lo_ok, 1)

            def y_copy(n, u, i):
                dve.wait_ge(y_mm, n + 1)
                wait_for(dve, y_st[u], 16 * i)
                dve.tensor_reduce(y_out[:, u, :], ps[:, 7, 0:2 * D].rearrange("p (h d) -> p d h", h=2), AX.X,
                                  ALU.add).then_inc(y_ok, 1)

            xe_low(0, 0)
            hidden(0, 0)
            xe_low(1, 1)
            hidden(1, 1)
            xe_low(2, 0)
            hT_low(0, 0)
            hidden(2, 0)
            xe_low(3, 1)
            hT_low(1, 1)
            y_copy(0, 0, 0)
            hidden(3, 1)
            with dve.Fori(2, MT // 2) as i:
                for u in range(2):
                    n = 2 * i + u
                    xe_low(n, u)
                    hT_low(n - 2, u)
                    y_copy(n - 3, 1 - u, i - 2 if u == 0 else i - 1)
                    hidden(n, u)
            hT_low(MT - 2, 0)
            y_copy(MT - 3, 1, MT // 2 - 2)
            hT_low(MT - 1, 1)
            y_copy(MT - 2, 0, MT // 2 - 1)
            y_copy(MT - 1, 1, MT // 2 - 1)

            def final_stats(g, u):
                dve.wait_ge(mixed, g + 1)
                wait_for(dve, f_kept, g - 1)
                for k in range(GT):
                    dve.bn_stats(fst[:, u, k, :], H[:, bass.ds(GT * g + k, 1), :]).then_inc(f_st, 1)
                wait_apart(dve, const_ok, (f_st, GT * g + GT))
                for k in range(GT):
                    dve.bn_aggr(mv[:, u, k, :], fst[:, u, k, :]).then_inc(f_mv, 1)
                dve.wait_ge(f_mv, GT * g + GT)
                dve.tensor_copy(fmv[:, bass.ds(GT * g, GT), :], mv[:, u, :, :]).then_inc(f_kept, 1)
            in_pairs(dve, 0, NG, final_stats)
            dve.wait_ge(f_kept, NG)
            dve.tensor_tensor(fa[:], prob[:, 0, :], prob[:, 0, :], ALU.mult).then_inc(f_s, 1)
            dve.wait_ge(f_s, 1)
            dve.tensor_tensor(fv[:], fa[:], fmv[:, :, 1], ALU.mult).then_inc(f_s, 1)
            dve.wait_ge(f_s, 2)
            dve.tensor_scalar(fv[:], fv[:], EPS, None, ALU.add).then_inc(f_s, 1)
            dve.wait_ge(f_rs, 1)
            dve.tensor_tensor(fa[:], prob[:, 0, :], fv[:], ALU.mult).then_inc(f_s, 1)
            dve.wait_ge(f_s, 4)
            dve.scalar_tensor_tensor(out=fb[:], in0=fmv[:, :, 0], scalar=-1.0, in1=fa[:],
                                     op0=ALU.mult, op1=ALU.mult).then_inc(f_s, 1)

            def finish(g, u):
                dve.wait_ge(f_n, GT * g + GT)
                dve.tensor_tensor(tiles4(tmp, u), tiles4(tmp, u), X[:, bass.ds(GT * g, GT), :],
                                  ALU.add).then_inc(f_ok, 1)
            in_pairs(dve, 0, NG, finish)


_INS = ['L0_attn_x', 'L0_attn_A', 'L0_attn_B_w', 'L0_attn_Wo', 'L0_attn_bo', 'L0_ffn_gate_w',
        'L0_ffn_wg', 'L0_ffn_wu', 'L0_ffn_wd']


def kernel(**inputs):
    import numpy as _np
    import concourse.bacc as _bacc
    from concourse import mybir as _mybir
    from concourse.bass_utils import run_bass_kernel_spmd as _run

    nc = _bacc.Bacc("TRN2", target_bir_lowering=False, num_devices=1)
    arrays, args = {}, []
    for name in _INS:
        a = _np.ascontiguousarray(inputs[name])
        arrays[f"in_{name}_dram"] = a
        args.append(nc.dram_tensor(f"in_{name}_dram", a.shape, _mybir.dt.from_np(a.dtype),
                                   kind="ExternalInput").ap())
    shape = inputs['L0_attn_x'].shape
    args.append(nc.dram_tensor("out_0_dram", shape, _mybir.dt.float32, kind="ExternalOutput").ap())
    build(nc, *args)
    r = _run(nc, [arrays], core_ids=[0])
    return r.results[0]["out_0_dram"]
```

```python
from contextlib import ExitStack

import concourse.bass as bass
from concourse import mybir

F32 = mybir.dt.float32
F32R = mybir.dt.float32r
BF16 = mybir.dt.bfloat16
I32 = mybir.dt.int32
U32 = mybir.dt.uint32
ALU = mybir.AluOpType
ACT = mybir.ActivationFunctionType
AX = mybir.AxisListType

P = 128
EPS = 1e-5


def wait_for(eng, sem, value):
    if isinstance(value, int) and value <= 0:
        return
    eng.wait_ge(sem, value)


def wait_apart(eng, settled, *waits):
    waits = [w for w in waits if not isinstance(w[1], int) or w[1] > 0]
    for _, value in waits:
        if not isinstance(value, int):
            eng.lower_val(value)
    eng.wait_ge(settled, 1)
    for sem, value in waits:
        eng.wait_ge(sem, value)


def in_pairs(eng, lo, hi, step):
    if lo == 0:
        step(0, 0)
        step(1, 1)
        lo = 2
    if lo < hi:
        with eng.Fori(lo // 2, hi // 2) as i:
            step(2 * i, 0)
            step(2 * i + 1, 1)


def build(nc, x, A, B_w, Wo, bo, gate_w, w_gate, w_up, w_down, out):
    NB, S, D = x.shape
    E, I, _ = w_gate.shape
    TPT = P // NB
    NT = S // TPT
    GT = 4
    NG = NT // GT
    NCH = 4
    GPC = NG // NCH
    IC = I // P
    NTOK = NT * P
    CAP = NTOK + P
    MT = 2 * NTOK // P + E
    XB = 4
    TPE = CAP // P
    SPARE = E * CAP
    ROWS = SPARE + E * P
    assert D == P and NB * TPT == P and NG % 2 == 0 and MT % XB == 0 and XB % 2 == 0 and I == GT * P

    x_sorted = nc.dram_tensor("x_sorted", [ROWS, D], F32, kind="Internal").ap()
    y_listed = nc.dram_tensor("y_listed", [MT * P, D], F32, kind="Internal").ap()

    ctx = ExitStack()
    with ctx:
        def sb(name, shape, dt=F32):
            return ctx.enter_context(nc.sbuf_tensor(name, shape, dt))

        def sem(name):
            return ctx.enter_context(nc.semaphore(name))

        ps = ctx.enter_context(nc.psum_tensor("ps", [P, 8, 512], F32))

        X = sb("X", [P, NT, D])
        H = sb("H", [P, NT, P])
        W = sb("W", [P, 3 * E * IC * 2 * P], F32R)

        ident = sb("ident", [P, P])
        below = sb("below", [P, P], BF16)
        ones_bf = sb("ones_bf", [P, P], BF16)
        ones_f = sb("ones_f", [P, P])
        below_f = sb("below_f", [E, E])
        half = sb("half", [P, 2 * GT])
        expert_id = sb("expert_id", [P, GT, E])
        expert_row = sb("expert_row", [P, GT, E])
        tile_no = sb("tile_no", [P, MT])
        eighths = sb("eighths", [1, 1, XB])
        ecol = sb("ecol", [E, 2])
        tail_row = sb("tail_row", [P, E])
        decay = sb("decay", [P, 1])
        a_col = sb("a_col", [P, 1])
        bo_row = sb("bo_row", [1, D])
        bo_parts = sb("bo_parts", [1, 2, D], F32R)
        ones_r = sb("ones_r", [1, P], F32R)
        BwT, WoT = sb("BwT", [P, P]), sb("WoT", [P, P])
        gateT = sb("gateT", [P, E])
        gate_in = sb("gate_in", [E, P])

        wstage = sb("wstage", [P, 2, 512])
        xT = sb("xT", [P, 2, 512])
        tmp = sb("tmp", [P, 2, 512])
        small_w = tmp[:, 1, 0:2 * P].rearrange("p (a i) -> p a i", a=2)
        xh2 = sb("xh2", [P, 2, 512])
        hid = sb("hid", [P, 2, 512])
        hT_hi, hT_lo = sb("hT_hi", [P, 2, 512], F32R), sb("hT_lo", [P, 2, 512], F32R)
        xeT_hi, xeT_lo = sb("xeT_hi", [P, 2, P], F32R), sb("xeT_lo", [P, 2, P], F32R)
        y_out = sb("y_out", [P, 2, D])
        xe = wstage[:, 0, :].rearrange("p (b d) -> p b d", b=XB)
        xn, xnT = xT[:, 1, :], xT[:, 0, :]
        st = sb("st", [P, 2, 2 * GT, 6])
        mv = sb("mv", [P, 2, 2 * GT, 2])
        ve = sb("ve", [P, 2, 2 * GT])
        rs = sb("rs", [P, 2, 2 * GT])
        nmr = sb("nmr", [P, 2, 2 * GT])
        root_t = sb("root_t", [P, 2 * GT])
        st1 = sb("st1", [P, 2, GT, 6])
        mv1 = sb("mv1", [P, 2, GT, 2])
        ve1, rs1, nmr1 = sb("ve1", [P, 2, GT]), sb("rs1", [P, 2, GT]), sb("nmr1", [P, 2, GT])
        mx = sb("mx", [P, 2, GT, 8])
        mi = sb("mi", [P, 2, GT, 8], U32)
        oh = sb("oh", [P, 2, 2, GT, E])
        mem = sb("mem", [P, 2, GT, E], BF16)
        gsum = sb("gsum", [P, 2, E])
        msum = sb("msum", [P, 2, E], BF16)
        rank = sb("rank", [P, 2, GT, E])
        sel = sb("sel", [P, 2, 2, GT, E])
        pos = sb("pos", [P, 2, NT], I32)
        pos_w = sb("pos_w", [P, 2, 2, GT], I32)
        margin = sb("margin", [P, NT])
        th = sb("th", [P, NT])
        prob = sb("prob", [P, 2, NT])
        tail = sb("tail", [P, E], I32)
        tiles_of = sb("tiles_of", [P, E])
        tiles_e = sb("tiles_e", [E, 1])
        tiles_i = sb("tiles_i", [E, 1], I32)
        level = sb("level", [E, TPE])
        level_at = sb("level_at", [TPE, 1])
        total = sb("total", [1, 3])
        la, lb, lc, ld = (hid[0:n, h // 2, MT * (h % 2):MT * (h % 2) + MT] for h, n in enumerate((TPE, E, E, 1)))
        rows = sb("rows", [1, MT], I32)
        experts = sb("experts", [1, MT // XB], I32)
        pk = sb("pk", [1, 2, MT // XB])
        place_i = sb("place_i", [P, 2 * NT], I32)
        place_t, place_e, place_n = (sb("place_" + n, [P, 2 * NT]) for n in ("t", "e", "n"))
        pos_y = sb("pos_y", [P, 2, NT], I32)
        last_i = sb("last_i", [P, NG], I32)
        ratio = sb("ratio", [P, NT])
        p1sq = sb("p1sq", [P, NT])
        mean, root = place_e[:, 0:NT], place_e[:, NT:2 * NT]
        fa, fb, fv = sb("fa", [P, NT]), sb("fb", [P, NT]), sb("fv", [P, NT])
        tail_i = sb("tail_i", [P, E], I32)
        zero = sb("zero", [P, D])

        x_in = [sem(f"x_in{c}") for c in range(NCH)]
        small_in, w_in0, w_in1 = sem("small_in"), sem("w_in0"), sem("w_in1")
        w_in = (w_in0, w_in1)
        pool_k, const_ok = sem("pool_k"), sem("const_ok")
        prep_t, prep_c, bo_ok = sem("prep_t"), sem("prep_c"), sem("bo_ok")
        w_t, w_hi_ok, w_lo_ok = sem("w_t"), sem("w_hi_ok"), sem("w_lo_ok")
        ln1_st, ln1_mv, ln1_ve, ln1_rs, ln1_nm, ln1_x = (sem("ln1_" + n) for n in ("st", "mv", "ve", "rs", "nm", "x"))
        ln1_x3 = sem("ln1_x3")
        ln1_t, ln1_xT, bx_mm, bx_ok = sem("ln1_t"), sem("ln1_xT"), sem("bx_mm"), sem("bx_ok")
        u_ok, h_ok = sem("u_ok"), sem("h_ok")
        o_mm, o_st, o_mv, o_n, x1_ok = (sem("o_" + n) for n in ("mm", "st", "mv", "n", "x1"))
        ve_ok, rs_ok, nm_ok, root_ok = sem("ve_ok"), sem("rs_ok"), sem("nm_ok"), sem("root_ok")
        l2_st, l2_mv, l2_x, l2_t, l2_xT, rows_ok = (sem("l2_" + n) for n in ("st", "mv", "x", "t", "xT", "rows"))
        lg_mm, mx_ok, mi_ok, mg_ok, oh_ok, mem_ok, gs_ok, ms_ok = (
            sem(n) for n in ("lg_mm", "mx_ok", "mi_ok", "mg_ok", "oh_ok", "mem_ok", "gs_ok", "ms_ok"))
        rk_mm, rk_ok, sel_ok, pos_ok = (sem(n) for n in ("rk_mm", "rk_ok", "sel_ok", "pos_ok"))
        y_zero = sem("y_zero")
        pos_kept, pos_back = sem("pos_kept"), sem("pos_back")
        scat = [sem("scat0"), sem("scat1")]
        tl, pl, wide = sem("tl"), sem("pl"), sem("wide")
        fill_ok = sem("fill_ok")
        c_mm, l_ok = sem("c_mm"), sem("l_ok")
        l_mm, tiles_ok, tail_ok, tailed = sem("l_mm"), sem("tiles_ok"), sem("tail_ok"), sem("tailed")
        xe_in = [sem(f"xe_in{b}") for b in range(XB)]
        xe_t, xe_hi, xe_lo = sem("xe_t"), sem("xe_hi"), sem("xe_lo")
        gu_mm, silu_ok, hid_ok, hT_t, hT_hi_ok, hT_lo_ok = (
            sem(n) for n in ("gu_mm", "silu_ok", "hid_ok", "hT_t", "hT_hi_ok", "hT_lo_ok"))
        y_mm, y_ok = sem("y_mm"), sem("y_ok")
        y_st = [sem("y_st0"), sem("y_st1")]
        th_ok, pr_r, pr_ok = sem("th_ok"), sem("pr_r"), sem("pr_ok")
        gath = [sem("gath0"), sem("gath1")]
        f_kept = sem("f_kept")
        mix_a, mixed = sem("mix_a"), sem("mixed")
        mix_late, mixed_late = sem("mix_late"), sem("mixed_late")
        f_st, f_mv, f_s, f_v, f_rt, f_nw, f_co, f_n, f_ok = (
            sem("f_" + n) for n in ("st", "mv", "s", "v", "rt", "nw", "co", "n", "ok"))
        f_ok_pool, out_ok = sem("f_ok_pool"), sem("out_ok")

        CONSTANTS = 14 + XB
        NW = 3 * E

        def tiles4(buf, u):
            return buf[:, u, :].rearrange("p (k d) -> p k d", k=GT)

        def parts(n):
            both = W[:, bass.ds(n * 2 * I, 2 * I)].rearrange("p (k h i) -> p k h i", k=IC, h=2)
            return [both[:, :, h, :] for h in range(2)]

        def valid(g):
            return not isinstance(g, int) or 0 <= g < NG

        LAST = 5
        W0, W1 = 2, 2 + NW // 2

        def tile_exists(n):
            return not isinstance(n, int) or 0 <= n < MT

        STATS_AT = 104

        def in_turns(eng, body):
            for n in range(4):
                body(n, n % 2)
            with eng.Fori(2, STATS_AT // 2) as i:
                body(2 * i, 0)
                body(2 * i + 1, 1)
            for n in range(STATS_AT, STATS_AT + 14):
                body(n, n % 2)
            with eng.Fori(STATS_AT // 2 + 7, MT // 2 - 1) as i:
                body(2 * i, 0)
                body(2 * i + 1, 1)
            for n in range(MT - 2, MT + 3):
                body(n, n % 2)

        def in_rounds(eng, body):
            for c in range(LAST + 1):
                body(c, c % 2)
            with eng.Fori((LAST + 1) // 2, NG // 2 - 1) as i:
                body(2 * i, 0)
                body(2 * i + 1, 1)
            for c in range(NG - 2, NG + LAST):
                body(c, c % 2)

        assert W1 == NG - 2 and TPT * GT == 16

        AHEAD = GPC
        LATE = NG - AHEAD

        def stage(c, s):
            m = (GT * c + s // 4) if isinstance(c, int) else LATE + 3
            return m, s % 4

        def late(m):
            return 0 <= m < LATE

        def over(c):
            return isinstance(c, int) and c >= NG

        def loads_weights(c):
            return not isinstance(c, int) or W0 <= c < W1

        def splits_weights(c):
            return not isinstance(c, int) or W0 < c < W1 + 1

        batches = ((0, 3), (3, 6), (6, 9), (9, 12), (12, 14), (14, 16))
        BY_DVE = 12
        POOL_BATCHES, dve_batches = [0, 1, 2], [3, 4, 5]
        assert batches[-1][1] == NG and 4 * GT == 16

        block = ctx.enter_context(nc.Block())

        @block.sync
        def _(sp):
            for c in range(NCH):
                for s in range(TPT):
                    sp.dma_start(X[s * NB:(s + 1) * NB, c * (NT // NCH):(c + 1) * (NT // NCH), :],
                                 x[:, c * (S // NCH) + s:(c + 1) * (S // NCH):TPT, :]).then_inc(x_in[c], 16)
                if c == 0:
                    sp.dma_start(small_w[:, 0, :], B_w).then_inc(small_in, 16)
                    sp.dma_start(small_w[:, 1, :], Wo).then_inc(small_in, 16)
                    sp.dma_start(gate_in[:], gate_w).then_inc(small_in, 16)
                    sp.dma_start(bo_row[:], bo.rearrange("(a d) -> a d", a=1)).then_inc(small_in, 16)
                    sp.dma_start(a_col[:], A.rearrange("(d a) -> d a", a=1)).then_inc(small_in, 16)
            sp.wait_ge(const_ok, CONSTANTS)

            def fill(k):
                sp.dma_start(y_listed[bass.ds(k * E * P, E * P), :].rearrange("(a p) d -> p a d", p=P),
                             zero[:].rearrange("p (a d) -> p a d", a=1).broadcast_to([P, E, D])
                             ).then_inc(y_zero, 16)
            for which, w in enumerate((w_gate, w_up, w_down)):
                def load(e, u, which=which, w=w):
                    n = which * E + e
                    wait_for(sp, w_t, n - 1)
                    if which < 2:
                        src = w[bass.ds(e, 1), :, :].rearrange("a (k p) d -> p (a k) d", p=P)
                    else:
                        src = w[bass.ds(e, 1), :, :].rearrange("a d (k i) -> d (a k) i", i=P)
                    sp.dma_start(tiles4(wstage, u), src).then_inc(w_in[u], 16)
                    if which > 0:
                        fill(n - E)
                if which == 0:
                    load(0, 0)
                    load(1, 1)
                with sp.Fori(1 if which == 0 else 0, E // 2) as i:
                    load(2 * i, 0)
                    load(2 * i + 1, 1)
            fill(2 * E)
            sp.dma_start(x_sorted[SPARE:ROWS, :].rearrange("(a p) d -> p a d", p=P),
                         zero[:].rearrange("p (a d) -> p a d", a=1).broadcast_to([P, E, D])).then_inc(fill_ok, 16)
            assert MT == (2 * E + 1) * E
            sp.wait_ge(tail_ok, 1)
            for e in range(E):
                row = sp.value_load(tail[0:1, e:e + 1], min_val=0, max_val=ROWS - P)
                sp.dma_start(x_sorted[bass.ds(row, P), :], zero[:]).then_inc(tailed, 16)
            sp.wait_ge(w_t, NW)
            sp.wait_ge(tiles_ok, 1)
            sp.wait_ge(tailed, 16 * E)
            sp.wait_ge(fill_ok, 16)
            for u in range(2):
                sp.wait_ge(scat[u], 16 * 2 * GT * NG // 2)

            def rows_of(n):
                return sp.value_load(rows[0:1, bass.ds(n, 1)], min_val=0, max_val=ROWS - P)

            def load_rows(n, b):
                wait_for(sp, xe_t, n - XB + 1)
                sp.dma_start(xe[:, b, :], x_sorted[bass.ds(rows_of(n), P), :]).then_inc(xe_in[b], 16)

            def store_rows(n, u):
                sp.wait_ge(y_ok, n + 1)
                sp.dma_start(y_listed[bass.ds(n * P, P), :], y_out[:, u, :]).then_inc(y_st[u], 16)

            sp.wait_ge(y_zero, 16 * (MT // E))
            for b in range(XB):
                load_rows(b, b)
            for b in range(XB):
                load_rows(XB + b, b)
            with sp.Fori(2, MT // XB) as i:
                for b in range(XB):
                    load_rows(XB * i + b, b)
                    store_rows(XB * i + b - 2 * XB, b % 2)
            for b in range(2 * XB):
                store_rows(MT - 2 * XB + b, b % 2)

            order = POOL_BATCHES + dve_batches
            for b in order:
                g0, g1 = batches[b]
                if b in POOL_BATCHES:
                    sp.wait_ge(f_ok_pool, g1)
                else:
                    sp.wait_ge(f_ok, g1 - batches[dve_batches[0]][0])
                for s in range(TPT):
                    sp.dma_start(out[:, g0 * GT * TPT + s:g1 * GT * TPT:TPT, :],
                                 H[s * NB:(s + 1) * NB, GT * g0:GT * g1, :]).then_inc(out_ok, 16)
            sp.wait_ge(out_ok, 16 * TPT * len(batches))

        @block.gpsimd
        def _(pool):
            pool.memset(ident[:], 0.0).then_inc(pool_k, 1)
            pool.memset(below[:], 0.0).then_inc(pool_k, 1)
            pool.memset(below_f[:], 0.0).then_inc(pool_k, 1)
            pool.memset(ones_bf[:], 1.0).then_inc(const_ok, 1)
            pool.memset(ones_f[:], 1.0).then_inc(const_ok, 1)
            pool.memset(half[:], -0.5).then_inc(const_ok, 1)
            pool.memset(zero[:], 0.0).then_inc(const_ok, 1)
            pool.memset(msum[:], 0.0).then_inc(const_ok, 1)
            pool.wait_ge(pool_k, 3)
            pool.affine_select(out=ident[:], in_=ident[:], compare_op=ALU.not_equal, fill=1.0, base=0,
                               pattern=[[-1, P]], channel_multiplier=1).then_inc(const_ok, 1)
            pool.affine_select(out=below[:], in_=below[:], compare_op=ALU.is_ge, fill=1.0, base=0,
                               pattern=[[-1, P]], channel_multiplier=1).then_inc(const_ok, 1)
            pool.affine_select(out=below_f[:], in_=below_f[:], compare_op=ALU.is_ge, fill=1.0, base=0,
                               pattern=[[-1, E]], channel_multiplier=1).then_inc(const_ok, 1)
            iota = dict(allow_small_or_imprecise_dtypes=True)
            pool.iota(expert_id[:], [[0, GT], [1, E]], base=0, channel_multiplier=0, **iota).then_inc(const_ok, 1)
            pool.iota(expert_row[:], [[0, GT], [CAP, E]], base=0, channel_multiplier=0, **iota).then_inc(const_ok, 1)
            pool.iota(tile_no[:], [[1, MT]], base=0, channel_multiplier=0, **iota).then_inc(const_ok, 1)
            pool.iota(ecol[:, 0:1], [[0, 1]], base=0, channel_multiplier=1, **iota).then_inc(const_ok, 1)
            pool.iota(ecol[:, 1:2], [[0, 1]], base=0, channel_multiplier=CAP, **iota).then_inc(const_ok, 1)
            pool.iota(tail_row[:], [[CAP, E]], base=0, channel_multiplier=1, **iota).then_inc(const_ok, 1)
            for b in range(XB):
                pool.memset(eighths[:, :, b], 8.0 ** b).then_inc(const_ok, 1)
            pool.wait_ge(const_ok, CONSTANTS)

            def ln1(g, u):
                pool.wait_ge(ln1_ve, g + 1)
                wait_for(pool, ln1_x, 3 * (g - 1))
                wait_for(pool, ln1_x3, g - 1)
                pool.tensor_tensor(rs1[:, u, :], ve1[:, u, :], half[:, 0:GT], ALU.pow).then_inc(ln1_rs, 1)
            in_pairs(pool, 0, AHEAD, ln1)

            def in_round(c, u):
                def late_powers(blocks):
                    for j in blocks:
                        m, _ = stage(c, 4 * j)
                        if late(m):
                            ln1(AHEAD + m, m % 2)
                late_powers([0])
                if (valid(c - 2) or valid(c - 3)) and not over(c):
                    a, b = (0 if valid(c - 2) else GT), (2 * GT if valid(c - 3) else GT)
                    pool.wait_ge(ve_ok, c - 1)
                    wait_for(pool, o_n, GT * (c - 3))
                    wait_for(pool, l2_x, GT * (c - 4))
                    pool.tensor_tensor(rs[:, 1 - u, a:b], ve[:, 1 - u, a:b], half[:, a:b], ALU.pow).then_inc(rs_ok, 1)
                late_powers([1, 2, 3])
                if valid(c - 5):
                    wait_apart(pool, const_ok, (pos_ok, c - 4), (rows_ok, c - 4))
                    for k in range(GT):
                        for w in range(2):
                            pool.indirect_dma_start(
                                out=x_sorted, out_offset=bass.IndirectOffsetOnAxis(
                                    ap=pos_w[:, 1 - u, w, k:k + 1], axis=0),
                                in_=xh2[:, 1 - u, k * P:(k + 1) * P], in_offset=None,
                                bounds_check=ROWS - 1, oob_is_err=False).then_inc(scat[1 - u], 16)
            in_rounds(pool, in_round)

            steps = [0]

            def chained(ins):
                steps[0] += 1
                ins.then_inc(pl, 1)
                pool.wait_ge(pl, steps[0])

            va, vb = xT[:, 0, 0:2 * NT], xT[:, 0, 2 * NT:4 * NT]
            flat = pos[:].rearrange("p c t -> p (c t)")
            pool.wait_ge(pos_kept, NG)
            for u in range(2):
                pool.wait_ge(scat[u], 16 * 2 * GT * NG // 2)
            pool.wait_ge(wide, 1)
            chained(pool.tensor_scalar(place_i[:], flat, 1.0 / P, (P - 1) / (2.0 * P), ALU.mult, ALU.subtract))
            chained(pool.tensor_copy(place_t[:], place_i[:]))
            chained(pool.memset(place_e[:], 0.0))
            for e in range(1, E):
                chained(pool.tensor_scalar(va, place_t[:], float(e * TPE), None, ALU.is_ge))
                chained(pool.tensor_tensor(place_e[:], place_e[:], va, ALU.add))
            chained(pool.tensor_scalar(va, place_e[:], float(TPE), None, ALU.mult))
            chained(pool.tensor_tensor(vb, place_t[:], va, ALU.subtract))
            chained(pool.memset(place_n[:], 0.0))
            for e in range(E):
                chained(pool.tensor_scalar(va, place_e[:], float(e), None, ALU.is_gt))
                chained(pool.tensor_tensor(va, va, vb, ALU.add))
                chained(pool.tensor_scalar(va, va, tiles_of[:, e:e + 1], None, ALU.min))
                chained(pool.tensor_tensor(place_n[:], place_n[:], va, ALU.add))
            chained(pool.partition_all_reduce(place_e[:], place_n[:], P, bass.bass_isa.ReduceOp.max))
            width = 2 * NT
            while width > NG:
                if width == 2 * NT:
                    one, two = place_e[:, 0:NT], place_e[:, NT:2 * NT]
                else:
                    one, two = (place_e[:, 0:width].rearrange("p (n h) -> p n h", h=2)[:, :, h] for h in range(2))
                width //= 2
                chained(pool.tensor_tensor(va[:, 0:width], two, one, ALU.subtract))
                chained(pool.tensor_scalar(va[:, 0:width], va[:, 0:width], 0.0, None, ALU.max))
                chained(pool.tensor_tensor(vb[:, 0:width], va[:, 0:width], one, ALU.add))
                chained(pool.tensor_copy(place_e[:, 0:width], vb[:, 0:width]))
            chained(pool.tensor_scalar(last_i[:], place_e[:, 0:NG], 0.5, 0.25, ALU.mult, ALU.subtract))
            chained(pool.tensor_tensor(place_n[:], place_n[:], place_t[:], ALU.subtract))
            chained(pool.tensor_scalar(place_n[:], place_n[:], float(P), None, ALU.mult))
            chained(pool.tensor_copy(place_i[:], place_n[:]))
            chained(pool.tensor_tensor(pos_y[:].rearrange("p c t -> p (c t)"), place_i[:], flat, ALU.add))
            pool.wait_ge(pr_ok, 3)

            def gather(g, u):
                half_last = pool.value_load(last_i[0:1, bass.ds(g, 1)], min_val=0, max_val=MT // 2 - 1)
                wait_apart(pool, const_ok, (y_st[0], half_last * 16 + 16), (y_st[1], half_last * 16 + 16),
                           (gath[u], 8 * 2 * GT * (g - u)),
                           (mixed, min(g - 1, BY_DVE) if isinstance(g, int) else g - 1),
                           (mixed_late, g - 1 - BY_DVE if isinstance(g, int) else 0))
                pool.tensor_copy(pos_w[:, u, :, :], pos_y[:, :, bass.ds(GT * g, GT)]).then_inc(pos_back, 1)
                wait_apart(pool, const_ok, (pos_back, g + 1))
                for k in range(GT):
                    for c, buf in enumerate((xh2, xT)):
                        pool.indirect_dma_start(
                            out=buf[:, u, k * P:(k + 1) * P], out_offset=None, in_=y_listed,
                            in_offset=bass.IndirectOffsetOnAxis(ap=pos_w[:, u, c, k:k + 1], axis=0),
                            bounds_check=MT * P - 1, oob_is_err=False).then_inc(gath[u], 16)

            def mix(g, u):
                pool.wait_ge(gath[u], 8 * 2 * GT * (g - u) + 16 * 2 * GT)
                pool.tensor_tensor(tiles4(xT, u), tiles4(xT, u),
                                   ratio[:, bass.ds(GT * g, GT)].rearrange("p (k a) -> p k a", a=1)
                                   .broadcast_to([P, GT, D]), ALU.mult).then_inc(mix_a, 1)
                pool.wait_ge(mix_a, g + 1)
                pool.tensor_tensor(H[:, bass.ds(GT * g, GT), :], tiles4(xT, u), tiles4(xh2, u),
                                   ALU.add).then_inc(mixed, 1)

            gather(0, 0)
            gather(1, 1)
            mix(0, 0)
            with pool.Fori(1, BY_DVE // 2) as i:
                gather(2 * i, 0)
                mix(2 * i - 1, 1)
                gather(2 * i + 1, 1)
                mix(2 * i, 0)
            gather(BY_DVE, 0)
            mix(BY_DVE - 1, 1)
            for g in range(BY_DVE + 1, NG):
                gather(g, g % 2)

            def finish(g):
                pool.wait_ge(f_n, GT * g + GT)
                rows_h = H[:, bass.ds(GT * g, GT), :]
                pool.tensor_tensor(rows_h, rows_h, X[:, bass.ds(GT * g, GT), :], ALU.add).then_inc(f_ok_pool, 1)
            with pool.Fori(0, batches[POOL_BATCHES[-1]][1]) as g:
                finish(g)

        @block.tensor
        def _(pe):
            pe.wait_ge(const_ok, CONSTANTS)
            pe.wait_ge(small_in, 16 * 5)
            pe.transpose(ps[:, 0, 0:P], small_w[:, 0, :], ident[:])
            pe.transpose(ps[:, 0, P:2 * P], small_w[:, 1, :], ident[:])
            pe.transpose(ps[:, 0, 2 * P:2 * P + E], gate_in[:], ident[0:E, 0:E]).then_inc(prep_t, 1)
            def ln1(g, u):
                pe.wait_ge(ln1_x, 3 * g + 3)
                pe.wait_ge(ln1_x3, g + 1)
                wait_for(pe, ln1_xT, g - 1)
                for k in range(GT):
                    last = pe.transpose(ps[:, 4 + 3 * u, k * P:(k + 1) * P], xh2[:, u, k * P:(k + 1) * P], ident[:])
                last.then_inc(ln1_t, 1)
            in_pairs(pe, 0, AHEAD, ln1)

            def bx_group(g):
                wait_for(pe, bx_ok, g)
                if isinstance(g, int):
                    pe.wait_ge(ln1_xT, g + 1)
                pe.matmul(tiles4(ps, 0), BwT[:], H[:, bass.ds(GT * g, GT), :], start=True, stop=True).then_inc(bx_mm, 1)
            pe.wait_ge(prep_c, 4)
            pe.wait_ge(bo_ok, 3)
            bx_group(0)

            def in_round(c, u):
                def late_transposes(j):
                    m, _ = stage(c, 4 * j)
                    if late(m - 2):
                        ln1(AHEAD + m - 2, m % 2)
                if valid(c - 1):
                    pe.wait_ge(h_ok, TPT * GT * c)
                    wait_for(pe, o_n, GT * (c - 2))
                    for h in range(2):
                        pe.matmul(tiles4(ps, 3 - u), ones_r[:], bo_parts[:, h:h + 1, :].broadcast_to([1, GT, D]),
                                  start=h == 0, stop=False)
                    for k in range(GT):
                        last = pe.matmul(ps[:, 3 - u, k * P:(k + 1) * P], hid[:, 1 - u, k * P:(k + 1) * P],
                                         WoT[:], start=False, stop=k == GT - 1)
                    last.then_inc(o_mm, 1)
                late_transposes(0)
                late_transposes(1)
                if valid(c - 5):
                    pe.wait_ge(mem_ok, c - 4)
                    wait_for(pe, ms_ok, c - 5)
                    rk = ps[:, 7, 64:64 + GT * E].rearrange("p (k e) -> p k e", k=GT)
                    pe.matmul(rk, below[:], mem[:, 1 - u, :, :], start=True, stop=False)
                    pe.matmul(rk, ones_bf[:], msum[:, u:u + 1, :].broadcast_to([P, GT, E]),
                              start=False, stop=False)
                    for k in range(GT - 1):
                        last = pe.matmul(rk[:, k + 1:GT, :], ones_bf[:],
                                         mem[:, 1 - u, k:k + 1, :].broadcast_to([P, GT - 1 - k, E]),
                                         start=False, stop=k == GT - 2)
                    last.then_inc(rk_mm, 1)
                if valid(c - 4):
                    pe.wait_ge(l2_x, GT * (c - 3))
                    wait_for(pe, l2_xT, c - 4)
                    for k in range(GT):
                        last = pe.transpose(ps[:, 4, k * P:(k + 1) * P], xn[:, k * P:(k + 1) * P], ident[:])
                    last.then_inc(l2_t, 1)
                if valid(c) and valid(c + 1):
                    bx_group(c + 1)
                late_transposes(2)
                late_transposes(3)
                if valid(c - 4):
                    pe.wait_ge(l2_xT, c - 3)
                    wait_for(pe, rk_ok, c - 4)
                    for k in range(GT):
                        last = pe.matmul(ps[:, 7, k * E:(k + 1) * E], xnT[:, k * P:(k + 1) * P], gateT[:],
                                         start=True, stop=True)
                    last.then_inc(lg_mm, 1)
                if loads_weights(c):
                    for w, bank in enumerate((1, 5)):
                        pe.wait_ge(w_in[w], 16 * (c - W0) + 16)
                        wait_for(pe, w_lo_ok, 2 * (c - W0) + w - 1)
                        for k in range(IC):
                            last = pe.transpose(ps[:, bank, k * P:(k + 1) * P],
                                                wstage[:, w, k * P:(k + 1) * P], ident[:])
                        last.then_inc(w_t, 1)
            in_rounds(pe, in_round)

            pe.wait_ge(ms_ok, NG)
            pe.wait_ge(rk_ok, NG)
            pe.wait_ge(bx_ok, NG)
            pe.wait_ge(o_n, GT * NG)
            pe.wait_ge(w_hi_ok, NW)
            pe.wait_ge(w_lo_ok, NW)
            pe.matmul(ps[0:E, 0, 0:1], msum[:, 1, :], ones_bf[:, 0:1], start=True, stop=True)
            pe.matmul(ps[:, 0, E:2 * E], ones_bf[:], msum[:, 1, :], start=True, stop=True).then_inc(c_mm, 1)
            pe.wait_ge(l_ok, 2)
            pe.matmul(ps[0:TPE, 1, 0:1], level[:], ones_f[0:E, 0:1], start=True, stop=True)
            pe.matmul(ps[0:1, 1, 2:3], ones_f[0:E, 0:1], tiles_e[:], start=True, stop=True).then_inc(l_mm, 1)
            pe.wait_ge(l_ok, 3)
            pe.matmul(ps[0:E, 2, 0:MT], ones_f[0:TPE, 0:E], la[:], start=True, stop=True).then_inc(l_mm, 1)
            pe.wait_ge(l_ok, 5)
            pe.matmul(ps[0:E, 3, 0:MT], ones_f[0:E, 0:E], lb[:], start=True, stop=False)
            pe.matmul(ps[0:E, 3, 0:MT], below_f[:], lc[:], start=False, stop=True).then_inc(l_mm, 1)
            pe.wait_ge(l_ok, 6)
            pe.matmul(ps[0:1, 1, 4:4 + MT], ones_f[0:E, 0:1], la[0:E, :], start=True, stop=True).then_inc(l_mm, 1)
            pe.wait_ge(tiles_ok, 1)

            def t_x(n, b, i):
                pe.wait_ge(xe_in[b], 16 * i + 16)
                wait_for(pe, xe_hi, n)
                wait_for(pe, xe_lo, n)
                pe.transpose(ps[:, 6, 0:P], xe[:, b, :], ident[:]).then_inc(xe_t, 1)

            def experts_of(i):
                packed = pe.value_load(experts[0:1, bass.ds(i, 1)], min_val=0, max_val=E ** (2 * XB - 1) - 1)
                return [(packed // E ** j) % E for j in range(2 * XB - 1)]

            assert E == 8
            def gate_up(n, u, e):
                pe.wait_ge(xe_hi, n + 1)
                pe.wait_ge(xe_lo, n + 1)
                wait_for(pe, hid_ok, n - 1)
                for b, n_w in ((0, e), (2, E + e)):
                    acc = tiles4(ps, b + u)
                    hi, lo = parts(n_w)
                    pe.matmul(acc, xeT_hi[:, u, :], hi, start=True, stop=False)
                    pe.matmul(acc, xeT_hi[:, u, :], lo, start=False, stop=False)
                    last = pe.matmul(acc, xeT_lo[:, u, :], hi, start=False, stop=True)
                last.then_inc(gu_mm, 1)

            def t_h(n, u):
                pe.wait_ge(hid_ok, n + 1)
                wait_for(pe, hT_hi_ok, n - 1)
                wait_for(pe, hT_lo_ok, n - 1)
                for k in range(IC):
                    last = pe.transpose(ps[:, 4 + u, k * P:(k + 1) * P], hid[:, u, k * P:(k + 1) * P], ident[:])
                last.then_inc(hT_t, 1)

            def down(n, u, e):
                pe.wait_ge(hT_hi_ok, n + 1)
                pe.wait_ge(hT_lo_ok, n + 1)
                wait_for(pe, y_ok, n)
                for k in range(IC):
                    h, l = hT_hi[:, u, k * P:(k + 1) * P], hT_lo[:, u, k * P:(k + 1) * P]
                    pe.matmul(ps[:, 7, 0:2 * D], h, W[:, bass.ds(((2 * E + e) * IC + k) * 2 * D, 2 * D)],
                              start=k == 0, stop=False, skip_group_check=True)
                    last = pe.matmul(ps[:, 7, 0:D], l, W[:, bass.ds(((2 * E + e) * IC + k) * 2 * D, D)],
                                     start=False, stop=k == IC - 1, skip_group_check=True)
                last.then_inc(y_mm, 1)

            def in_turn(n, b, listed, i):
                if tile_exists(n + 1):
                    t_x(n + 1, (b + 1) % XB, i + 1 if b == XB - 1 else i)
                if tile_exists(n - 2):
                    t_h(n - 2, b % 2)
                if tile_exists(n - 3):
                    down(n - 3, 1 - b % 2, listed[b])
                if tile_exists(n):
                    gate_up(n, b % 2, listed[b + 3])

            t_x(0, 0, 0)
            listed = experts_of(0)
            for b in range(XB):
                in_turn(b, b, listed, 0)
            with pe.Fori(1, MT // XB - 1) as i:
                listed = experts_of(i)
                for b in range(XB):
                    in_turn(XB * i + b, b, listed, i)
            listed = experts_of(MT // XB - 1)
            for b in range(XB):
                in_turn(MT - XB + b, b, listed, MT // XB - 1)
            for b in range(3):
                in_turn(MT + b, b, listed[XB:], MT // XB)

        @block.scalar
        def _(act):
            def ln1_copy(g, u):
                act.wait_ge(ln1_t, g + 1)
                act.copy(H[:, bass.ds(GT * g, GT), :], tiles4(ps, 4 + 3 * u)).then_inc(ln1_xT, 1)

            def ln1_norm(g, u, k):
                if k == 0:
                    act.wait_ge(ln1_nm, g + 1)
                    wait_for(act, ln1_t, g - 1)
                act.activation(xh2[:, u, k * P:(k + 1) * P], X[:, bass.ds(GT * g + k, 1), :], ACT.Identity,
                               bias=nmr1[:, u, k:k + 1], scale=rs1[:, u, k:k + 1]).then_inc(ln1_x, 1)

            def ln1(g, u):
                for k in range(3):
                    ln1_norm(g, u, k)
                if not isinstance(g, int) or g > 0:
                    ln1_copy(g - 1, 1 - u)
            in_pairs(act, 0, AHEAD, ln1)
            ln1_copy(AHEAD - 1, 1)
            act.wait_ge(prep_c, 4)
            act.activation(decay[:], a_col[:], ACT.Exp, scale=-1.0).then_inc(prep_c, 1)

            def bx_copy(g, u):
                act.wait_ge(bx_mm, g + 1)
                wait_for(act, o_mm, g - 1)
                act.copy(hid[:, u, :], ps[:, 0, :]).then_inc(bx_ok, 1)
            bx_copy(0, 0)

            def in_round(c, u):
                def step(s):
                    if valid(c):
                        act.wait_ge(u_ok, TPT * GT * c + s + 1)
                        act.activation(hid[:, u, s * NB:(s + 1) * NB], ps[:, 6, (s % 2) * NB:(s % 2 + 1) * NB],
                                       ACT.Tanh).then_inc(h_ok, 1)
                    m, part = stage(c, s)
                    if part >= 2 and late(m - 1):
                        ln1_norm(AHEAD + m - 1, (m - 1) % 2, part - 2)
                    if part == 0 and late(m - 2):
                        ln1_norm(AHEAD + m - 2, m % 2, 2)
                    if part == 1 and late(m - 3):
                        ln1_copy(AHEAD + m - 3, (m - 3) % 2)

                def high(w, bank):
                    if splits_weights(c):
                        n = 2 * (c - 1 - W0) + w
                        act.wait_ge(w_t, n + 1)
                        act.copy(parts(n)[0], tiles4(ps, bank)).then_inc(w_hi_ok, 1)

                def x_norm(k):
                    g, v = (c - 3, 1 - u) if k < 2 else (c - 4, u)
                    if valid(g):
                        act.wait_ge(nm_ok, g + 2)
                        wait_for(act, l2_t, g)
                        wait_for(act, rows_ok, g)
                        act.activation(xn[:, k * P:(k + 1) * P], X[:, bass.ds(GT * g + k, 1), :], ACT.Identity,
                                       bias=nmr[:, v, GT + k:GT + k + 1],
                                       scale=rs[:, v, GT + k:GT + k + 1]).then_inc(l2_x, 1)

                def o_norm(k):
                    if valid(c - 2):
                        if k == 0:
                            act.wait_ge(nm_ok, c - 1)
                            wait_for(act, x1_ok, 2 * (c - 3))
                        act.activation(tmp[:, u, k * P:(k + 1) * P], ps[:, 2 + u, k * P:(k + 1) * P], ACT.Identity,
                                       bias=nmr[:, 1 - u, k:k + 1], scale=rs[:, 1 - u, k:k + 1]).then_inc(o_n, 1)

                def x_transposed():
                    if valid(c - 4):
                        act.wait_ge(l2_t, c - 3)
                        wait_for(act, lg_mm, c - 4)
                        act.copy(xnT[:], ps[:, 4, :]).then_inc(l2_xT, 1)

                def rows_copy():
                    if valid(c - 4):
                        act.wait_ge(l2_x, GT * (c - 3))
                        wait_for(act, scat[u], 8 * 2 * GT * (c - 4 - u))
                        act.copy(xh2[:, u, :], xn).then_inc(rows_ok, 1)

                step(0)
                x_norm(2)
                step(1)
                x_norm(3)
                step(2)
                high(0, 1)
                step(3)
                high(1, 5)
                step(4)
                step(5)
                step(6)
                x_transposed()
                step(7)
                step(8)
                if valid(c) and valid(c + 1):
                    bx_copy(c + 1, 1 - u)
                step(9)
                o_norm(0)
                step(10)
                o_norm(1)
                step(11)
                o_norm(2)
                step(12)
                o_norm(3)
                step(13)
                rows_copy()
                step(14)
                x_norm(0)
                step(15)
                x_norm(1)
            in_rounds(act, in_round)

            act.wait_ge(mg_ok, NG)
            act.activation(th[:], margin[:], ACT.Tanh, scale=0.5).then_inc(th_ok, 1)

            def xe_high(n, u):
                act.wait_ge(xe_t, n + 1)
                wait_for(act, gu_mm, n - 1)
                act.copy(xeT_hi[:, u, :], ps[:, 6, 0:P]).then_inc(xe_hi, 1)

            def silu(n, u):
                act.wait_ge(gu_mm, n + 1)
                wait_for(act, hid_ok, n - 1)
                act.activation(tmp[:, u, :], ps[:, u, :], ACT.Silu).then_inc(silu_ok, 1)

            def hT_high(n, u):
                act.wait_ge(hT_t, n + 1)
                wait_for(act, y_mm, n - 1)
                act.copy(hT_hi[:, u, :], ps[:, 4 + u, :]).then_inc(hT_hi_ok, 1)

            def in_turn(n, u):
                if tile_exists(n - 1):
                    silu(n - 1, 1 - u)
                if tile_exists(n + 1):
                    xe_high(n + 1, 1 - u)
                if tile_exists(n - 2):
                    hT_high(n - 2, u)
            xe_high(0, 0)
            in_turns(act, in_turn)

            def final_root(b):
                t0, t1 = (GT * g for g in batches[b])
                act.wait_ge(f_v, b + 1)
                act.activation(root[:, t0:t1], fv[:, t0:t1], ACT.Sqrt).then_inc(f_rt, 1)

            def final_norm(b, h):
                g0, g1 = batches[b]
                n = GT * (g1 - g0) // 2
                if h == 0:
                    act.wait_ge(f_co, b + 1)
                for j in range(GT * g0 + h * n, GT * g0 + (h + 1) * n):
                    act.activation(H[:, j, :], H[:, j, :], ACT.Identity,
                                   bias=fb[:, j:j + 1], scale=fa[:, j:j + 1]).then_inc(f_n, 1)
            final_root(0)
            for b in range(len(batches)):
                final_norm(b, 0)
                if b + 1 < len(batches):
                    final_root(b + 1)
                final_norm(b, 1)

        @block.vector
        def _(dve):
            dve.wait_ge(const_ok, CONSTANTS)

            def ln1_bias(g, u):
                dve.wait_ge(ln1_rs, g + 1)
                wait_for(dve, ln1_x, 3 * (g - 1))
                dve.scalar_tensor_tensor(out=nmr1[:, u, :], in0=mv1[:, u, :, 0], scalar=-1.0,
                                         in1=rs1[:, u, :], op0=ALU.mult, op1=ALU.mult).then_inc(ln1_nm, 1)

            def ln1_stats(g, u, tiles):
                for k in tiles:
                    dve.bn_stats(st1[:, u, k, :], X[:, bass.ds(GT * g + k, 1), :]).then_inc(ln1_st, 1)

            def ln1_variance(g, u):
                wait_apart(dve, const_ok, (ln1_st, GT * g + GT), (ln1_nm, g - 1))
                for k in range(GT):
                    dve.bn_aggr(mv1[:, u, k, :], st1[:, u, k, :]).then_inc(ln1_mv, 1)
                dve.wait_ge(ln1_mv, GT * g + GT)
                wait_for(dve, ln1_rs, g - 1)
                dve.tensor_scalar(ve1[:, u, :], mv1[:, u, :, 1], EPS, None, ALU.add).then_inc(ln1_ve, 1)

            def ln1_last(g, u):
                k = GT - 1
                dve.wait_ge(ln1_nm, g + 1)
                wait_for(dve, ln1_t, g - 1)
                dve.tensor_scalar(xh2[:, u, k * P:(k + 1) * P], X[:, bass.ds(GT * g + k, 1), :],
                                  rs1[:, u, k:k + 1], nmr1[:, u, k:k + 1], ALU.mult, ALU.add).then_inc(ln1_x3, 1)

            def ln1(g, u):
                ln1_stats(g, u, range(GT))
                ln1_variance(g, u)
                if not isinstance(g, int) or g > 0:
                    ln1_bias(g - 1, 1 - u)
                    ln1_last(g - 1, 1 - u)
            dve.wait_ge(x_in[0], 16 * TPT)
            in_pairs(dve, 0, AHEAD, ln1)
            dve.wait_ge(small_in, 16 * 5)
            dve.tensor_scalar(a_col[:], a_col[:], 10.0, None, ALU.min).then_inc(prep_c, 1)
            dve.wait_ge(prep_t, 1)
            dve.tensor_copy(BwT[:], ps[:, 0, 0:P]).then_inc(prep_c, 1)
            dve.tensor_copy(WoT[:], ps[:, 0, P:2 * P]).then_inc(prep_c, 1)
            dve.tensor_copy(gateT[:], ps[:, 0, 2 * P:2 * P + E]).then_inc(prep_c, 1)
            dve.tensor_copy(ones_r[:], ones_f[0:1, :]).then_inc(bo_ok, 1)
            dve.tensor_copy(bo_parts[:, 0, :], bo_row[:]).then_inc(bo_ok, 1)
            dve.wait_ge(bo_ok, 2)
            dve.tensor_tensor(bo_parts[:, 1, :], bo_row[:], bo_parts[:, 0, :].bitcast(F32),
                              ALU.subtract).then_inc(bo_ok, 1)
            ln1_bias(AHEAD - 1, 1)
            ln1_last(AHEAD - 1, 1)
            dve.wait_ge(prep_c, 5)

            root_steps = [0]

            def in_round(c, u):
                def step(s):
                    if not valid(c):
                        return
                    dst = ps[:, 6, (s % 2) * NB:(s % 2 + 1) * NB]
                    if s == 0:
                        dve.wait_ge(bx_ok, c + 1)
                    if s == 0 and isinstance(c, int) and c == 0:
                        dve.tensor_copy(dst, hid[:, 0, 0:NB]).then_inc(u_ok, 1)
                        return
                    dve.wait_ge(h_ok, TPT * GT * c + s)
                    before = hid[:, u, (s - 1) * NB:s * NB] if s else hid[:, 1 - u, 512 - NB:512]
                    dve.scalar_tensor_tensor(out=dst, in0=before, scalar=decay[:, 0:1],
                                             in1=hid[:, u, s * NB:(s + 1) * NB],
                                             op0=ALU.mult, op1=ALU.add).then_inc(u_ok, 1)

                chain_step = step

                def step(s):
                    chain_step(s)
                    m, part = stage(c, s)
                    if late(m) and part < 2:
                        g = AHEAD + m
                        if part == 0 and g % GPC == 0:
                            dve.wait_ge(x_in[g // GPC], 16 * TPT)
                        ln1_stats(g, m % 2, (2 * part, 2 * part + 1))
                    if late(m - 1) and part == 1:
                        ln1_bias(AHEAD + m - 1, (m - 1) % 2)
                    if late(m - 1) and part == 3:
                        ln1_last(AHEAD + m - 1, (m - 1) % 2)
                    if late(m) and part == 2:
                        ln1_variance(AHEAD + m, m % 2)

                def ranked():
                    if valid(c - 5):
                        v = 1 - u
                        dve.wait_ge(rk_mm, c - 4)
                        dve.tensor_tensor(rank[:, v, :, :],
                                          ps[:, 7, 64:64 + GT * E].rearrange("p (k e) -> p k e", k=GT),
                                          expert_row[:], ALU.add).then_inc(rk_ok, 1)

                def select():
                    if valid(c - 5):
                        v = 1 - u
                        dve.wait_ge(rk_ok, c - 4)
                        dve.tensor_tensor(sel[:, v, :, :, :], oh[:, v, :, :, :],
                                          rank[:, v:v + 1, :, :].broadcast_to([P, 2, GT, E]),
                                          ALU.mult).then_inc(sel_ok, 1)

                def placed():
                    if valid(c - 5):
                        v = 1 - u
                        dve.wait_ge(sel_ok, c - 4)
                        wait_for(dve, scat[v], 8 * 2 * GT * (c - 5 - v))
                        with nc.allow_low_precision(reason="whole numbers below 2^24"):
                            dve.tensor_reduce(pos_w[:, v, :, :], sel[:, v, :, :, :], AX.X, ALU.add).then_inc(pos_ok, 1)

                def kept():
                    if valid(c - 5):
                        dve.wait_ge(pos_ok, c - 4)
                        dve.tensor_copy(pos[:, :, bass.ds(GT * (c - 5), GT)], pos_w[:, 1 - u, :, :]
                                        ).then_inc(pos_kept, 1)

                def bias():
                    if valid(c - 2) or valid(c - 3):
                        a, b = (0 if valid(c - 2) else GT), (2 * GT if valid(c - 3) else GT)
                        dve.wait_ge(rs_ok, c - 1)
                        dve.scalar_tensor_tensor(out=nmr[:, 1 - u, a:b], in0=mv[:, 1 - u, a:b, 0], scalar=-1.0,
                                                 in1=rs[:, 1 - u, a:b], op0=ALU.mult, op1=ALU.mult
                                                 ).then_inc(nm_ok, 1)

                def low(w, bank):
                    if splits_weights(c):
                        n = 2 * (c - 1 - W0) + w
                        dve.wait_ge(w_hi_ok, n + 1)
                        hi, lo = parts(n)
                        dve.tensor_tensor(lo, tiles4(ps, bank), hi.bitcast(F32), ALU.subtract).then_inc(w_lo_ok, 1)

                def add_x(h):
                    if valid(c - 2):
                        dve.wait_ge(o_n, GT * (c - 2) + 2 * h + 2)
                        rows_x = X[:, bass.ds(GT * (c - 2) + 2 * h, 2), :]
                        dve.tensor_tensor(rows_x, rows_x, tiles4(tmp, u)[:, 2 * h:2 * h + 2, :],
                                          ALU.add).then_inc(x1_ok, 1)

                def o_stats(k):
                    if valid(c - 1):
                        if k == 0:
                            wait_apart(dve, const_ok, (o_mm, c))
                        dve.bn_stats(st[:, u, k, :], ps[:, 3 - u, k * P:(k + 1) * P]).then_inc(o_st, 1)

                def x1_stats(k):
                    g, v = (c - 2, u) if k < 2 else (c - 3, 1 - u)
                    if valid(g):
                        if k == 0:
                            wait_apart(dve, const_ok, (x1_ok, 2 * (g + 1)))
                        dve.bn_stats(st[:, v, GT + k, :], X[:, bass.ds(GT * g + k, 1), :]).then_inc(l2_st, 1)

                def o_aggr():
                    if valid(c - 1):
                        wait_apart(dve, const_ok, (o_st, GT * c))
                        for k in range(GT):
                            dve.bn_aggr(mv[:, u, k, :], st[:, u, k, :]).then_inc(o_mv, 1)

                def x1_aggr():
                    if valid(c - 3):
                        wait_apart(dve, const_ok, (l2_st, GT * (c - 2)))
                        for k in range(GT):
                            dve.bn_aggr(mv[:, 1 - u, GT + k, :], st[:, 1 - u, GT + k, :]).then_inc(l2_mv, 1)

                def variances():
                    if valid(c - 2) or valid(c - 3):
                        a, b = (0 if valid(c - 2) else GT), (2 * GT if valid(c - 3) else GT)
                        if valid(c - 2):
                            dve.wait_ge(o_mv, GT * (c - 1))
                        if valid(c - 3):
                            dve.wait_ge(l2_mv, GT * (c - 2))
                        dve.tensor_scalar(ve[:, 1 - u, a:b], mv[:, 1 - u, a:b, 1], EPS, None, ALU.add
                                          ).then_inc(ve_ok, 1)
                        if over(c):
                            inverse_root(a, b)

                def inverse_root(a, b):
                    v, r, t = ve[:, 1 - u, a:b], rs[:, 1 - u, a:b], root_t[:, a:b]

                    def then(ins):
                        root_steps[0] += 1
                        ins.then_inc(root_ok, 1)
                        dve.wait_ge(root_ok, root_steps[0])
                    dve.wait_ge(ve_ok, c - 1)
                    dve.wait_ge(o_n, GT * min(c - 3, NG))
                    dve.wait_ge(l2_x, GT * (c - 4))
                    then(dve.tensor_scalar(r.bitcast(I32), v.bitcast(I32), -0.5, float(0x5f3759df),
                                           ALU.mult, ALU.add))
                    for _ in range(2):
                        then(dve.tensor_tensor(t, r, r, ALU.mult))
                        then(dve.scalar_tensor_tensor(out=t, in0=t, scalar=-0.5, in1=v, op0=ALU.mult, op1=ALU.mult))
                        then(dve.scalar_tensor_tensor(out=r, in0=t, scalar=1.5, in1=r, op0=ALU.add, op1=ALU.mult))
                    then(dve.tensor_tensor(t, r, r, ALU.mult))
                    then(dve.scalar_tensor_tensor(out=t, in0=t, scalar=-0.5, in1=v, op0=ALU.mult, op1=ALU.mult))
                    dve.scalar_tensor_tensor(out=r, in0=t, scalar=1.5, in1=r, op0=ALU.add, op1=ALU.mult
                                             ).then_inc(rs_ok, 1)

                lg = ps[:, 7, 0:GT * E].rearrange("p (k e) -> p k e", k=GT)

                def largest():
                    if valid(c - 4):
                        wait_apart(dve, const_ok, (lg_mm, c - 3))
                        for k in range(GT):
                            dve.max(out=mx[:, u, k, :], in_=lg[:, k, :]).then_inc(mx_ok, 1)

                def chosen():
                    if valid(c - 4):
                        wait_apart(dve, const_ok, (mx_ok, GT * (c - 3)))
                        for k in range(GT):
                            dve.max_index(mi[:, u, k, :], mx[:, u, k, :], lg[:, k, :]).then_inc(mi_ok, 1)
                        dve.tensor_tensor(margin[:, bass.ds(GT * (c - 4), GT)], mx[:, u, :, 0], mx[:, u, :, 1],
                                          ALU.subtract).then_inc(mg_ok, 1)

                def one_hot():
                    if valid(c - 5):
                        v = 1 - u
                        dve.wait_ge(mi_ok, GT * (c - 4))
                        best = mi[:, v, :, 0:2].rearrange("p k (w e) -> p w k e", e=1)
                        dve.tensor_tensor(oh[:, v, :, :, :],
                                          expert_id[:].rearrange("p (w k) e -> p w k e", w=1)
                                          .broadcast_to([P, 2, GT, E]),
                                          best.broadcast_to([P, 2, GT, E]), ALU.is_equal).then_inc(oh_ok, 1)

                def members():
                    if valid(c - 5):
                        v = 1 - u
                        dve.wait_ge(oh_ok, c - 4)
                        dve.tensor_tensor(mem[:, v, :, :], oh[:, v, 0, :, :], oh[:, v, 1, :, :],
                                          ALU.add).then_inc(mem_ok, 1)

                def counts():
                    if valid(c - 5):
                        dve.wait_ge(mem_ok, c - 4)
                        dve.tensor_reduce(gsum[:, 1 - u, :], mem[:, 1 - u, :, :].rearrange("p k e -> p e k"), AX.X,
                                          ALU.add).then_inc(gs_ok, 1)

                def summed():
                    if valid(c - 5):
                        v = 1 - u
                        dve.wait_ge(gs_ok, c - 4)
                        wait_for(dve, ms_ok, c - 5)
                        wait_for(dve, rk_mm, c - 5)
                        dve.tensor_tensor(msum[:, v, :], gsum[:, v, :], msum[:, 1 - v, :], ALU.add).then_inc(ms_ok, 1)

                step(0)
                x1_stats(2)
                one_hot()
                step(1)
                x1_stats(3)
                members()
                step(2)
                x1_aggr()
                counts()
                step(3)
                variances()
                step(4)
                summed()
                ranked()
                step(5)
                o_stats(0)
                select()
                step(6)
                placed()
                o_stats(1)
                step(7)
                o_stats(2)
                bias()
                step(8)
                o_stats(3)
                low(0, 1)
                step(9)
                kept()
                o_aggr()
                step(10)
                low(1, 5)
                step(11)
                add_x(0)
                step(12)
                largest()
                step(13)
                add_x(1)
                step(14)
                chosen()
                step(15)
                x1_stats(0)
                x1_stats(1)
            in_rounds(dve, in_round)

            steps = [0]

            def chained(ins):
                steps[0] += 1
                ins.then_inc(tl, 1)
                dve.wait_ge(tl, steps[0])

            dve.wait_ge(c_mm, 1)
            dve.tensor_tensor(tail[:], ps[:, 0, E:2 * E], tail_row[:], ALU.add).then_inc(tail_ok, 1)
            chained(dve.tensor_scalar(tiles_i[:], ps[0:E, 0, 0:1], float(P - 1), None, ALU.add))
            chained(dve.tensor_single_scalar(tiles_i[:], tiles_i[:], 7, ALU.arith_shift_right))
            dve.tensor_copy(tiles_e[:], tiles_i[:]).then_inc(l_ok, 1)
            dve.wait_ge(l_ok, 1)
            dve.tensor_scalar(level[:], tile_no[0:E, 0:TPE], tiles_e[:, 0:1], None, ALU.min).then_inc(l_ok, 1)
            chained(dve.tensor_scalar(tail_i[:], ps[:, 0, E:2 * E], float(P - 1), None, ALU.add))
            chained(dve.tensor_single_scalar(tail_i[:], tail_i[:], 7, ALU.arith_shift_right))
            dve.tensor_copy(tiles_of[:], tail_i[:]).then_inc(wide, 1)
            dve.wait_ge(l_mm, 1)
            chained(dve.tensor_copy(total[:, 0:1], ps[0:1, 1, 2:3]))
            chained(dve.tensor_copy(level_at[:], ps[0:TPE, 1, 0:1]))
            dve.tensor_scalar(la[:], tile_no[0:TPE, :], level_at[:, 0:1], None, ALU.is_ge).then_inc(l_ok, 1)
            dve.wait_ge(l_mm, 2)
            dve.tensor_scalar(lb[:], ps[0:E, 2, 0:MT], -1.0, tiles_e[:, 0:1], ALU.add, ALU.min).then_inc(l_ok, 1)
            dve.tensor_scalar(lc[:], ps[0:E, 2, 0:MT], -1.0, tiles_e[:, 0:1], ALU.add, ALU.is_lt).then_inc(l_ok, 1)
            chained(dve.tensor_scalar(ld[:], ps[0:1, 2, 0:MT], float(P), -float(P), ALU.mult, ALU.add))
            dve.wait_ge(l_mm, 3)
            dve.tensor_tensor(la[0:E, :], ps[0:E, 3, 0:MT], tile_no[0:E, :], ALU.is_le).then_inc(l_ok, 1)
            chained(dve.tensor_scalar(total[:, 1:2], total[:, 0:1], -float(P), float(SPARE), ALU.mult, ALU.add))
            chained(dve.tensor_scalar(lb[0:1, :], tile_no[0:1, :], float(P), total[:, 1:2], ALU.mult, ALU.add))
            chained(dve.tensor_scalar(lc[0:1, :], tile_no[0:1, :], total[:, 0:1], None, ALU.is_lt))
            chained(dve.tensor_tensor(ld[:], ld[:], lb[0:1, :], ALU.subtract))
            dve.wait_ge(l_mm, 4)
            chained(dve.tensor_scalar(la[0:1, :], ps[0:1, 1, 4:4 + MT], -1.0, None, ALU.add))
            chained(dve.scalar_tensor_tensor(out=ld[:], in0=la[0:1, :], scalar=float(CAP), in1=ld[:],
                                             op0=ALU.mult, op1=ALU.add))
            chained(dve.tensor_tensor(ld[:], ld[:], lc[0:1, :], ALU.mult))
            chained(dve.tensor_tensor(rows[:], ld[:], lb[0:1, :], ALU.add))
            four = la[0:1, :].rearrange("p (i b) -> p i b", b=XB)
            chained(dve.tensor_tensor(ld[:].rearrange("p (i b) -> p i b", b=XB), four,
                                      eighths[:].broadcast_to([1, MT // XB, XB]), ALU.mult))
            chained(dve.tensor_reduce(pk[:, 0, :], ld[:].rearrange("p (i b) -> p i b", b=XB), AX.X, ALU.add))
            chained(dve.tensor_tensor(pk[:, 1, :], pk[:, 0, :], four[:, :, 0], ALU.subtract))
            chained(dve.tensor_scalar(pk[:, 1, :], pk[:, 1, :], 1.0 / E, None, ALU.mult))
            chained(dve.tensor_scalar(pk[:, 0, :], pk[:, 0, :], float(E ** 3), None, ALU.mult))
            chained(dve.tensor_copy(experts[:, 0:1], pk[:, 0, 0:1]))
            dve.tensor_tensor(experts[:, 1:], pk[:, 0, 1:], pk[:, 1, 0:MT // XB - 1], ALU.add).then_inc(tiles_ok, 1)

            dve.wait_ge(th_ok, 1)
            dve.tensor_scalar(prob[:, 0, :], th[:], 0.5, 0.5, ALU.mult, ALU.add).then_inc(pr_ok, 1)
            dve.tensor_scalar(prob[:, 1, :], th[:], -0.5, 0.5, ALU.mult, ALU.add).then_inc(pr_ok, 1)
            dve.wait_ge(pr_ok, 2)
            dve.reciprocal(ratio[:], prob[:, 0, :]).then_inc(pr_r, 1)
            dve.wait_ge(pr_r, 1)
            dve.tensor_tensor(ratio[:], ratio[:], prob[:, 1, :], ALU.mult).then_inc(pr_ok, 1)

            def xe_low(n, u):
                dve.wait_ge(xe_hi, n + 1)
                wait_for(dve, gu_mm, n - 1)
                dve.tensor_tensor(xeT_lo[:, u, :], ps[:, 6, 0:P], xeT_hi[:, u, :].bitcast(F32),
                                  ALU.subtract).then_inc(xe_lo, 1)

            def hidden(n, u):
                dve.wait_ge(silu_ok, n + 1)
                wait_for(dve, hT_t, n - 1)
                dve.tensor_tensor(hid[:, u, :], tmp[:, u, :], ps[:, 2 + u, :], ALU.mult).then_inc(hid_ok, 1)

            def hT_low(n, u):
                dve.wait_ge(hT_hi_ok, n + 1)
                wait_for(dve, y_mm, n - 1)
                dve.tensor_tensor(hT_lo[:, u, :], ps[:, 4 + u, :], hT_hi[:, u, :].bitcast(F32),
                                  ALU.subtract).then_inc(hT_lo_ok, 1)

            def y_copy(n, u):
                dve.wait_ge(y_mm, n + 1)
                wait_for(dve, y_st[u], 8 * (n - u))
                dve.tensor_reduce(y_out[:, u, :], ps[:, 7, 0:2 * D].rearrange("p (h d) -> p d h", h=2), AX.X,
                                  ALU.add).then_inc(y_ok, 1)

            dve.tensor_tensor(p1sq[:], prob[:, 0, :], prob[:, 0, :], ALU.mult).then_inc(f_s, 1)
            st_all = st[:].rearrange("p u k s -> p (u k) s")
            mv_all = mv[:].rearrange("p u k s -> p (u k) s")

            def final_ready(b):
                if batches[b][0] < BY_DVE:
                    dve.wait_ge(mixed, batches[b][1])
                else:
                    dve.wait_ge(mixed_late, batches[b][1] - BY_DVE)

            def final_tile(b, j):
                dve.bn_stats(st_all[:, j - GT * batches[b][0], :], H[:, j, :]).then_inc(f_st, 1)

            def final_means(b):
                t0, t1 = (GT * g for g in batches[b])
                wait_apart(dve, const_ok, (f_st, t1))
                for j in range(t0, t1):
                    dve.bn_aggr(mv_all[:, j - t0, :], st_all[:, j - t0, :]).then_inc(f_mv, 1)

            def final_variances(b):
                t0, t1 = (GT * g for g in batches[b])
                dve.wait_ge(f_mv, t1)
                dve.tensor_copy(mean[:, t0:t1], mv_all[:, 0:t1 - t0, 0]).then_inc(f_kept, 1)
                dve.tensor_tensor(fv[:, t0:t1], p1sq[:, t0:t1], mv_all[:, 0:t1 - t0, 1], ALU.mult).then_inc(f_s, 1)
                dve.wait_ge(f_s, 2 + b)
                dve.tensor_scalar(fv[:, t0:t1], fv[:, t0:t1], EPS, None, ALU.add).then_inc(f_v, 1)

            def final_stats(b, before=None):
                t0, t1 = (GT * g for g in batches[b])
                final_ready(b)
                for j in range(t0, t1):
                    final_tile(b, j)
                    if before is not None and j > t0:
                        final_factors(before, j - t0 - 1)
                final_means(b)
                final_variances(b)

            FIRST = GT * batches[0][1]
            assert STATS_AT - 4 >= E * FIRST and FIRST <= 12

            def in_turn(n, u):
                if tile_exists(n - 1):
                    hidden(n - 1, 1 - u)
                if tile_exists(n - 2):
                    hT_low(n - 2, u)
                if tile_exists(n + 1):
                    xe_low(n + 1, 1 - u)
                if tile_exists(n - 3):
                    y_copy(n - 3, 1 - u)
                if isinstance(n, int) and STATS_AT <= n < STATS_AT + 14:
                    k = n - STATS_AT
                    if k == 0:
                        final_ready(0)
                    if k < FIRST:
                        final_tile(0, k)
                    elif k == 12:
                        final_means(0)
                    elif k == 13:
                        final_variances(0)
            xe_low(0, 0)
            in_turns(dve, in_turn)

            def final_factors(b, i):
                t0, t1 = (GT * g for g in batches[b])
                r, q, v = root[:, t0:t1], fb[:, t0:t1], fv[:, t0:t1]
                if 0 < i < 7:
                    dve.wait_ge(f_nw, 6 * b + i)
                if i == 0:
                    dve.wait_ge(f_rt, b + 1)
                    dve.reciprocal(r, r).then_inc(f_nw, 1)
                elif i == 1:
                    dve.tensor_tensor(q, r, r, ALU.mult).then_inc(f_nw, 1)
                elif i == 2:
                    dve.tensor_tensor(q, q, v, ALU.mult).then_inc(f_nw, 1)
                elif i == 3:
                    dve.tensor_scalar(q, q, -0.5, 1.5, ALU.mult, ALU.add).then_inc(f_nw, 1)
                elif i == 4:
                    dve.tensor_tensor(r, r, q, ALU.mult).then_inc(f_nw, 1)
                elif i == 5:
                    dve.tensor_tensor(fa[:, t0:t1], prob[:, 0, t0:t1], r, ALU.mult).then_inc(f_nw, 1)
                elif i == 6:
                    dve.wait_ge(f_kept, b + 1)
                    dve.scalar_tensor_tensor(out=fb[:, t0:t1], in0=mean[:, t0:t1], scalar=-1.0, in1=fa[:, t0:t1],
                                             op0=ALU.mult, op1=ALU.mult).then_inc(f_co, 1)

            def finish(b):
                for g in range(*batches[b]):
                    dve.wait_ge(f_n, GT * g + GT)
                    rows_h = H[:, GT * g:GT * g + GT, :]
                    dve.tensor_tensor(rows_h, rows_h, X[:, GT * g:GT * g + GT, :], ALU.add).then_inc(f_ok, 1)

            def mix(g):
                u = g % 2
                dve.wait_ge(gath[u], 8 * 2 * GT * (g - u) + 16 * 2 * GT)
                dve.tensor_tensor(tiles4(xT, u), tiles4(xT, u),
                                  ratio[:, GT * g:GT * g + GT].rearrange("p (k a) -> p k a", a=1)
                                  .broadcast_to([P, GT, D]), ALU.mult).then_inc(mix_late, 1)
                dve.wait_ge(mix_late, g - BY_DVE + 1)
                dve.tensor_tensor(H[:, GT * g:GT * g + GT, :], tiles4(xT, u), tiles4(xh2, u),
                                  ALU.add).then_inc(mixed_late, 1)

            mix(12)
            for i in range(7):
                final_factors(0, i)
            final_stats(1)
            mix(13)
            final_stats(2, before=1)
            final_stats(3, before=2)
            final_stats(4, before=3)
            mix(14)
            mix(15)
            for i in range(7):
                final_factors(4, i)
            final_stats(5)
            for i in range(7):
                final_factors(5, i)
            finish(3)
            finish(4)
            finish(5)


_INS = ['L0_attn_x', 'L0_attn_A', 'L0_attn_B_w', 'L0_attn_Wo', 'L0_attn_bo', 'L0_ffn_gate_w',
        'L0_ffn_wg', 'L0_ffn_wu', 'L0_ffn_wd']


def kernel(**inputs):
    import numpy as _np
    import concourse.bacc as _bacc
    from concourse import mybir as _mybir
    from concourse.bass_utils import run_bass_kernel_spmd as _run

    nc = _bacc.Bacc("TRN2", target_bir_lowering=False, num_devices=1)
    arrays, args = {}, []
    for name in _INS:
        a = _np.ascontiguousarray(inputs[name])
        arrays[f"in_{name}_dram"] = a
        args.append(nc.dram_tensor(f"in_{name}_dram", a.shape, _mybir.dt.from_np(a.dtype),
                                   kind="ExternalInput").ap())
    shape = inputs['L0_attn_x'].shape
    args.append(nc.dram_tensor("out_0_dram", shape, _mybir.dt.float32, kind="ExternalOutput").ap())
    build(nc, *args)
    r = _run(nc, [arrays], core_ids=[0])
    return r.results[0]["out_0_dram"]
```
